# Optimizing a Trainium2 kernel written in Bass

```python
import numpy as np
import jax
import jax.numpy as jnp

def _softmax(x, axis=-1):
    return jax.nn.softmax(x, axis=axis)

def _gelu(x):
    return jax.nn.gelu(x, approximate=True)

def _silu(x):
    return jax.nn.silu(x)

def _sigmoid(x):
    return jax.nn.sigmoid(x)

def _layernorm(x, axis=-1, eps=1e-05):
    m = jnp.mean(x, axis=axis, keepdims=True)
    v = jnp.var(x, axis=axis, keepdims=True)
    return (x - m) / jnp.sqrt(v + eps)

def _scatter_add(tgt, idx, src, axis=0):
    return tgt.at[idx].add(src)

def _segment_sum(src, seg, n):
    return jax.ops.segment_sum(src, seg, n)
kernel_name = 'mk_flamingo_gated_d1_seqx_r8_08fc00'

def setup_inputs(seed: int=0):
    np.random.seed(seed)
    _w = jnp.asarray

    def _rec_inputs():
        import jax
        import jax.numpy as jnp
        _rk = jax.random.key(seed)
        x = 7.22e-05 + 1 * jax.random.normal(jax.random.fold_in(_rk, 1), (64, 128, 128), jnp.float32)
        _lenS = 128 - jax.random.randint(jax.random.fold_in(_rk, 7), (64,), 0, max(1, 128 // 4) + 1, jnp.int32)
        _lenS2 = 77 - jax.random.randint(jax.random.fold_in(_rk, 8), (64,), 0, max(1, 77 // 4) + 1, jnp.int32)
        _ctx_768P = jax.random.normal(jax.random.fold_in(_rk, 11), (64, 16, 96), jnp.float32)
        _ctx_768c = jax.random.dirichlet(jax.random.fold_in(_rk, 511), 0.3 * jnp.ones((16,), jnp.float32), (64, 77))
        _ctx_768t = jnp.einsum('bsk,bkd->bsd', _ctx_768c, _ctx_768P)
        _ctx_768t = _ctx_768t * jax.lax.rsqrt(jnp.mean(jnp.square(_ctx_768t)) + 1e-12) * 0.953939
        ctx_768 = -0.000191848 + 0.999787 * (_ctx_768t + 0.3 * jax.random.normal(jax.random.fold_in(_rk, 611), (64, 77, 96), jnp.float32))
        _g = jax.random.normal(jax.random.fold_in(_rk, 9001), (2, 1), jnp.float32)
        _g = jnp.sign(_g) * jnp.maximum(jnp.abs(_g), 1.0) + (_g == 0) * 1.0
        g_xattn = _g[0]
        g_ffn = _g[1]
        return (x, ctx_768, g_xattn, g_ffn)
    x, ctx_768, g_xattn, g_ffn = _rec_inputs()

    def _L0_xattn_setup():
        import jax, jax.numpy as jnp
        import numpy as np
        NUM_HEADS = 16
        CLAMP = 10000.0
        key = jax.random.key(seed)
        ks = jax.random.split(key, 8)
        B, Nq, Nkv, Cq, Ckv = (4, 256, 256, 128, 96)
        s_q = 1.0 / np.sqrt(Cq)
        s_kv = 1.0 / np.sqrt(Ckv)
        return {'query': jax.random.normal(ks[0], (B, Nq, Cq), jnp.float32), 'key_value': jax.random.normal(ks[1], (B, Nkv, Ckv), jnp.float32), 'Wq': jax.random.normal(ks[2], (Cq, Cq), jnp.float32) * s_q, 'bq': jnp.zeros((Cq,), jnp.float32), 'Wk': jax.random.normal(ks[3], (Ckv, Cq), jnp.float32) * s_kv, 'bk': jnp.zeros((Cq,), jnp.float32), 'Wv': jax.random.normal(ks[4], (Ckv, Cq), jnp.float32) * s_kv, 'bv': jnp.zeros((Cq,), jnp.float32), 'Wo': jax.random.normal(ks[5], (Cq, Cq), jnp.float32) * s_q, 'bo': jnp.zeros((Cq,), jnp.float32)}
    _L0_xattn_all = _L0_xattn_setup()
    _L0_xattn_in = {k: v for k, v in _L0_xattn_all.items() if k in ('Wq', 'bq', 'Wk', 'bk', 'Wv', 'bv', 'Wo', 'bo')}
    del _L0_xattn_all

    def _L0_ffn_setup():
        import jax, jax.numpy as jnp
        import numpy as np
        TOPK = 4
        key = jax.random.key(seed)
        ks = jax.random.split(key, 9)
        B, T, D = (4, 256, 128)
        E, H = (32, 128)
        HS = H * TOPK
        s = lambda k, shape, fan: jax.random.normal(k, shape, dtype=jnp.float32) / np.sqrt(fan)
        return {'x': jax.random.normal(ks[0], (B, T, D), dtype=jnp.float32), 'router_w': s(ks[1], (E, D), D), 'router_bias': jnp.zeros((E,), dtype=jnp.float32), 'gate_w': s(ks[2], (E, H, D), D), 'up_w': s(ks[3], (E, H, D), D), 'down_w': s(ks[4], (E, D, H), H), 'sgate_w': s(ks[5], (HS, D), D), 'sup_w': s(ks[6], (HS, D), D), 'sdown_w': s(ks[7], (D, HS), HS)}
    _L0_ffn_all = _L0_ffn_setup()
    _L0_ffn_in = {k: v for k, v in _L0_ffn_all.items() if k in ('router_w', 'router_bias', 'gate_w', 'up_w', 'down_w', 'sgate_w', 'sup_w', 'sdown_w')}
    del _L0_ffn_all
    return {'x': x, 'ctx_768': ctx_768, 'g_xattn': g_xattn, 'g_ffn': g_ffn, 'L0_xattn_Wq': _L0_xattn_in['Wq'], 'L0_xattn_bq': _L0_xattn_in['bq'], 'L0_xattn_Wk': _L0_xattn_in['Wk'], 'L0_xattn_bk': _L0_xattn_in['bk'], 'L0_xattn_Wv': _L0_xattn_in['Wv'], 'L0_xattn_bv': _L0_xattn_in['bv'], 'L0_xattn_Wo': _L0_xattn_in['Wo'], 'L0_xattn_bo': _L0_xattn_in['bo'], 'L0_ffn_router_w': _L0_ffn_in['router_w'], 'L0_ffn_router_bias': _L0_ffn_in['router_bias'], 'L0_ffn_gate_w': _L0_ffn_in['gate_w'], 'L0_ffn_up_w': _L0_ffn_in['up_w'], 'L0_ffn_down_w': _L0_ffn_in['down_w'], 'L0_ffn_sgate_w': _L0_ffn_in['sgate_w'], 'L0_ffn_sup_w': _L0_ffn_in['sup_w'], 'L0_ffn_sdown_w': _L0_ffn_in['sdown_w']}

def reference(x, ctx_768, g_xattn, g_ffn, L0_xattn_Wq, L0_xattn_bq, L0_xattn_Wk, L0_xattn_bk, L0_xattn_Wv, L0_xattn_bv, L0_xattn_Wo, L0_xattn_bo, L0_ffn_router_w, L0_ffn_router_bias, L0_ffn_gate_w, L0_ffn_up_w, L0_ffn_down_w, L0_ffn_sgate_w, L0_ffn_sup_w, L0_ffn_sdown_w):
    import jax
    import jax.numpy as jnp

    def _L0_xattn_ref(query, key_value, Wq, bq, Wk, bk, Wv, bv, Wo, bo):
        import jax, jax.numpy as jnp
        import numpy as np
        NUM_HEADS = 16
        CLAMP = 10000.0
        B, Nq, Cq = query.shape
        Nkv = key_value.shape[1]
        H = NUM_HEADS
        D = Cq // H
        scale = D ** (-0.5)
        q = (query @ Wq + bq).reshape(B, Nq, H, D).transpose(0, 2, 1, 3)
        k = (key_value @ Wk + bk).reshape(B, Nkv, H, D).transpose(0, 2, 1, 3)
        v = (key_value @ Wv + bv).reshape(B, Nkv, H, D).transpose(0, 2, 1, 3)
        attn = jnp.einsum('bhqd,bhkd->bhqk', q, k) * scale
        attn = jnp.clip(attn, -CLAMP, CLAMP)
        attn = jax.nn.softmax(attn, axis=-1)
        attn = jnp.where(jnp.any(jnp.isnan(attn)), jnp.asarray(1.0 / Nkv, attn.dtype), attn)
        x = jnp.einsum('bhqk,bhkd->bqhd', attn, v).reshape(B, Nq, Cq)
        return x @ Wo + bo

    def _L0_ffn_ref(x, router_w, router_bias, gate_w, up_w, down_w, sgate_w, sup_w, sdown_w):
        import jax, jax.numpy as jnp
        import numpy as np
        TOPK = 4
        B, T, D = x.shape
        flat = x.reshape(B * T, D)
        logits = flat.astype(jnp.float32) @ router_w.T + router_bias
        scores = jax.nn.softmax(logits, axis=-1)
        topk_scores, topk_idx = jax.lax.top_k(scores, TOPK)
        topk_scores = topk_scores / jnp.clip(topk_scores.sum(axis=-1, keepdims=True), 1e-12, None)
        h = jax.nn.silu(jnp.einsum('nd,ehd->neh', flat, gate_w)) * jnp.einsum('nd,ehd->neh', flat, up_w)
        expert_out = jnp.einsum('neh,edh->ned', h, down_w)
        sel = jnp.take_along_axis(expert_out, topk_idx[:, :, None], axis=1)
        out = (sel * topk_scores.astype(flat.dtype)[:, :, None]).sum(axis=1)
        out = out + jax.nn.silu(flat @ sgate_w.T) * (flat @ sup_w.T) @ sdown_w.T
        return out.reshape(B, T, D)
    x = x + jnp.tanh(g_xattn[0]) * _L0_xattn_ref(_layernorm(x, axis=-1), ctx_768, L0_xattn_Wq, L0_xattn_bq, L0_xattn_Wk, L0_xattn_bk, L0_xattn_Wv, L0_xattn_bv, L0_xattn_Wo, L0_xattn_bo)
    x = x + jnp.tanh(g_ffn[0]) * _L0_ffn_ref(_layernorm(x, axis=-1), L0_ffn_router_w, L0_ffn_router_bias, L0_ffn_gate_w, L0_ffn_up_w, L0_ffn_down_w, L0_ffn_sgate_w, L0_ffn_sup_w, L0_ffn_sdown_w)
    return x

_drawn_inputs = setup_inputs


def setup_inputs(seed=0):
    import zlib

    import numpy as np

    out = dict(_drawn_inputs(seed))
    spreads = {'L0_xattn_bq': (0.0, 0.1),
     'L0_xattn_bk': (0.0, 0.1),
     'L0_xattn_bv': (0.0, 0.1),
     'L0_xattn_bo': (0.0, 0.1),
     'L0_ffn_router_bias': (0.0, 0.1)}
    factors = {}
    for name, (base, spread) in spreads.items():
        noise = np.random.default_rng([zlib.crc32(name.encode()), seed]).standard_normal(out[name].shape)
        drawn = base * np.exp(spread * noise) if base else spread * noise
        out[name] = jnp.asarray(drawn.astype(out[name].dtype))
    for name, factor in factors.items():
        out[name] = (out[name] * factor).astype(out[name].dtype)
    return out
```

```python
from contextlib import ExitStack

import concourse.bass as bass
from concourse import mybir

F32 = mybir.dt.float32
BF16 = mybir.dt.bfloat16
U32 = mybir.dt.uint32
I32 = mybir.dt.int32
ALU = mybir.AluOpType
ACT = mybir.ActivationFunctionType
AX_X = mybir.AxisListType.X

B, T, D = 64, 128, 128
NKV, CKV = 77, 96
NH = 16
HD = D // NH
CLAMP = 10000.0
EPS = 1e-5
E, H = 32, 128
TOPK = 4
HS = 512
NS = HS // 128
TOKENS = B * T
ROW = D + 1
STRIDE = TOKENS + 128
DUMMY = E * STRIDE
XROWS = DUMMY + 128
TILES = 288
TGROUPS = 3
NOWHERE = 1 << 20

C_ID, C_TRI, C_ONE, C_IOTA, C_EOFF, C_J128, C_LOW = 0, 128, 256, 384, 416, 448, 512
C_T, C_DEST, C_PADD, C_END = 1536, 1539, 1543, 1544
W_Q, W_O, W_R, W_SG, W_SU, W_SD, W_END = 0, 128, 256, 288, 800, 1312, 1824
V_RB, V_BO, V_BV, V_BQ, V_BK, V_GX, V_GF, V_END = 0, 32, 160, 288, 289, 290, 291, 292
HEADS_PER_BANK = 512 // NKV
BANKS_S = [(h, min(h + HEADS_PER_BANK, NH)) for h in range(0, NH, HEADS_PER_BANK)]
PG = NH // 4


def build(nc, x, ctxT, wk, wv, wts, vecs, consts, gu, dn, out):
    x_rows = nc.dram_tensor("x_rows", (XROWS, ROW), F32).ap()
    y_rows = nc.dram_tensor("y_rows", (TOKENS * TOPK, D), F32).ap()
    table_dram = nc.dram_tensor("table_dram", (2, TGROUPS * 128), I32).ap()

    with ExitStack() as stack:
        def sb(name, shape, dt=F32):
            return stack.enter_context(nc.sbuf_tensor(name, shape, dt))

        def sem(name):
            return stack.enter_context(nc.semaphore(name))

        def sems(name, n=2):
            return [sem(f"{name}{i}") for i in range(n)]

        cst = sb("cst", [128, C_END])
        w = sb("w", [128, W_END])
        vec = sb("vec", [128, V_END])
        wk_sb = sb("wk_sb", [CKV, D])
        wv_sb = sb("wv_sb", [CKV, D])
        w_gu = sb("w_gu", [128, E * 2 * H])
        w_dn = sb("w_dn", [128, E * D])
        x_all = sb("x_all", [128, B * D])
        x2T_all = sb("x2T_all", [128, TOKENS])
        gates = sb("gates", [128, B * TOPK])
        tg = sb("tg", [128, 2])
        eps = sb("eps", [128, 1])
        bq_s = sb("bq_s", [128, 1])
        bias2 = sb("bias2", [128, D])
        tri = sb("tri", [128, 128], BF16)
        ones = sb("ones", [128, 128], BF16)
        base = sb("base", [128, 2, E])
        ident = cst[:, C_ID:C_ID + 128]
        iota = cst[:, C_IOTA:C_IOTA + E]

        ctx_sb = sb("ctx_sb", [CKV, 2, NKV])
        st1 = sb("st1", [128, 2, 6])
        mv1 = sb("mv1", [128, 2, 2])
        lv1 = sb("lv1", [128, 2])
        rs1 = sb("rs1", [128, 2])
        xn = sb("xn", [128, 2, D])
        xnT = sb("xnT", [128, 2, T])
        kT = sb("kT", [128, 2, NKV])
        kbd = sb("kbd", [128, 2, NH, NKV])
        qT = sb("qT", [128, 2, T])
        v9 = sb("v9", [NKV, 2, NH, HD + 1])
        mx = sb("mx", [128, NH])
        mxc = sb("mxc", [128, NH])
        prob = sb("prob", [128, 2, NH, NKV])
        pT = sb("pT", [NKV, PG, 4, T])
        rden = sb("rden", [128, NH])
        o_sb = sb("o_sb", [128, D])
        oT = sb("oT", [128, T])
        st2 = sb("st2", [128, 6])
        mv2 = sb("mv2", [128, 2])
        lv2 = sb("lv2", [128, 1])
        rs2 = sb("rs2", [128, 1])
        payload = sb("payload", [128, 2, TOPK, ROW])
        x2T = sb("x2T", [128, T])
        lg = sb("lg", [128, E])
        top = sb("top", [128, 8])
        ntop = sb("ntop", [128, 1])
        idx = sb("idx", [128, 8], U32)
        idxf = sb("idxf", [128, TOPK])
        onehot = sb("onehot", [128, TOPK, E], BF16)
        e4 = sb("e4", [128, TOPK])
        se4 = sb("se4", [128, 1])
        rse4 = sb("rse4", [128, 1])
        pos = sb("pos", [128, E])
        prod = sb("prod", [128, TOPK, E])
        slotf = sb("slotf", [128, TOPK])
        slot = sb("slot", [128, 2, TOPK], U32)
        dest = sb("dest", [128, 2, TOPK])

        cnt = sb("cnt", [128, E])
        cmpj = sb("cmpj", [128, E, 64])
        ntile = sb("ntile", [128, E])
        lowp = sb("lowp", [128, E, E])
        ends = sb("ends", [128, E])
        starts = sb("starts", [128, E])
        adj = sb("adj", [128, E])
        past = sb("past", [128, TGROUPS, E])
        et = sb("et", [128, TGROUPS])
        valid = sb("valid", [128, TGROUPS])
        oht = sb("oht", [128, TGROUPS, E])
        srow = sb("srow", [128, TGROUPS])
        trow = sb("trow", [128, TGROUPS])
        row2 = sb("row2", [128, TGROUPS])
        etc = sb("etc", [128, TGROUPS])
        tab = sb("tab", [128, 2, TGROUPS], I32)
        basei = sb("basei", [1, E], I32)
        tab_row = sb("tab_row", [1, 2 * TGROUPS * 128], I32)
        pad = sb("pad", [128, ROW])

        xin = sb("xin", [128, 4, ROW])
        xT = sb("xT", [128, 2, 128])
        sg = sb("sg", [128, 2, H])
        h = sb("h", [128, 2, H])
        hT = sb("hT", [128, 2, 128])
        y_sb = sb("y_sb", [128, 4, D])
        didx = sb("didx", [128, 4], U32)

        ssg = sb("ssg", [128, 2, 512])
        hs = sb("hs", [128, 2, 512])
        yld = w_gu[:, 0:4 * TOPK * D].rearrange("p (q k d) -> p q k d", q=4, k=TOPK)
        acc = w_gu[:, 4 * TOPK * D:4 * (TOPK + 2) * D].rearrange("p (q k d) -> p q k d", q=4, k=2)

        bank = [stack.enter_context(nc.psum_tensor(f"bank{i}", [128, 512], F32)) for i in range(8)]
        ps_s = bank[0:3]
        ps_p = bank[3:5]
        ps_o, ps_f, ps_b = bank[5], bank[6], bank[7]

        s_cst, s_w, s_vec, s_wkv, s_moe = sem("s_cst"), sem("s_w"), sem("s_vec"), sem("s_wkv"), sem("s_moe")
        s_x = sems("s_x", 4)
        s_zero, s_v1, s_tg, s_eps, s_bq, s_bvo, s_bias, s_b2g = (sem(n) for n in (
            "s_zero", "s_v1", "s_tg", "s_eps", "s_bq", "s_bvo", "s_bias", "s_b2g"))
        s_tri, s_base0, s_dest0, s_pad = sem("s_tri"), sem("s_base0"), sem("s_dest0"), sem("s_pad")
        ctx_in, kbd_in, sent = sems("ctx_in"), sems("kbd_in"), sems("sent")
        names = ("st1_d mv1_d lv1_d rs1_d xn_d xnT_p xnT_d k_p k_d q_p q_d v_p v_d s_p mx_d mxc_d diff_d relu_d "
                 "exp_d pt_p pt_d pv_p rden_d on_d oT_p oT_d y_p xb_d x1_d st2_d mv2_d lv2_d rs2_d x2_d x2T_p x2T_d "
                 "x2Ta_d lg_p lg_d top_d ntop_d idx_d idxf_d oh_d pre_p pos_d base_d prod_d slotf_d slot_d e4_d "
                 "rse_d gate_d pidx_d dest_d")
        S = {n: sem(n) for n in names.split()}
        (st1_d, mv1_d, lv1_d, rs1_d, xn_d, xnT_p, xnT_d, k_p, k_d, q_p, q_d, v_p, v_d, s_p, mx_d, mxc_d, diff_d,
         relu_d, exp_d, pt_p, pt_d, pv_p, rden_d, on_d, oT_p, oT_d, y_p, xb_d, x1_d, st2_d, mv2_d, lv2_d, rs2_d,
         x2_d, x2T_p, x2T_d, x2Ta_d, lg_p, lg_d, top_d, ntop_d, idx_d, idxf_d, oh_d, pre_p, pos_d, base_d, prod_d,
         slotf_d, slot_d, e4_d, rse_d, gate_d, pidx_d, dest_d) = S.values()
        t_step, t_tab, t_store, t_load, t_padded, t_basei = (sem(n) for n in (
            "t_step", "t_tab", "t_store", "t_load", "t_padded", "t_basei"))
        xin_in, y_sent = sems("xin_in", 4), sems("y_sent", 4)
        xT_p, xT_d, gu_p, sg_d, h_d, hT_p, hT_d, dn_p, y_d, didx_d = (sem(n) for n in (
            "xT_p", "xT_d", "gu_p", "sg_d", "h_d", "hT_p", "hT_d", "dn_p", "y_d", "didx_d"))
        yld_in, out_sent = sems("yld_in", 4), sems("out_sent", 4)
        sg_p, ssg_d, hs_d, sy_p, take_d, acc_d = (sem(n) for n in ("sg_p", "ssg_d", "hs_d", "sy_p", "take_d", "acc_d"))

        def need(eng, s, count):
            if not isinstance(count, int) or count > 0:
                eng.wait_ge(s, count)

        passed = sem("passed")

        def need_first(eng, s, count):
            need(eng, s, count)
            if not isinstance(count, int):
                eng.sem_inc(passed, 1)

        def pipeline(eng, step):
            for i in range(-2, 4):
                step(i, i % 2, lambda k, i=i: 0 <= i + k < B)
            with eng.Fori(2, B // 2 - 1) as j:
                for u in range(2):
                    step(2 * j + u, u, lambda k: True)
            for i in range(B - 2, B + 3):
                step(i, i % 2, lambda k, i=i: 0 <= i + k < B)

        def slot_uses(m, u):
            return (m - u) // 2 if isinstance(m, int) else None

        block = stack.enter_context(nc.Block())

        @block.sync
        def _(sp):
            sp.dma_start(cst[:, :], consts).then_inc(s_cst, 16)
            sp.dma_start(vec[:, :], vecs).then_inc(s_vec, 16)
            xv = x.rearrange("b t d -> t b d")
            for q in range(4):
                n = B // 4
                sp.dma_start(x_all[:, q * n * D:(q + 1) * n * D].rearrange("p (b d) -> p b d", d=D),
                             xv[:, q * n:(q + 1) * n, :]).then_inc(s_x[q], 16)
                if q == 0:
                    sp.dma_start(wk_sb[:, :], wk).then_inc(s_wkv, 16)
                    sp.dma_start(wv_sb[:, :], wv).then_inc(s_wkv, 16)
                    sp.dma_start(w[:, :], wts).then_inc(s_w, 16)

            def load_ctx(m, c, u):
                need(sp, v_p, m - 1)
                sp.dma_start(ctx_sb[:, u, :], ctxT[:, bass.ds(m * NKV, NKV)]).then_inc(ctx_in[u], 16)

            def spread_keys(m, u):
                need(sp, s_p, m - 1)
                need(sp, k_d, m + 1)
                for hh in range(NH):
                    sp.dma_start(kbd[HD * hh:HD * hh + HD, u, hh, :],
                                 kT[HD * hh:HD * hh + HD, u, :]).then_inc(kbd_in[u], 16)

            sp.wait_ge(s_zero, 1)

            def step(i, u, has):
                if has(2):
                    load_ctx(i + 2, None, u)
                if has(1):
                    spread_keys(i + 1, 1 - u)

            pipeline(sp, step)
            sp.dma_start(w_gu[:, :], gu).then_inc(s_moe, 16)
            sp.dma_start(w_dn[:, :], dn).then_inc(s_moe, 16)

            sp.wait_ge(s_pad, 3)
            sp.wait_ge(t_basei, 1)
            sp.dma_start(x_rows[DUMMY:DUMMY + 128, :], pad[:, :]).then_inc(t_padded, 16)
            with sp.Fori(0, E) as e:
                first = sp.value_load(basei[0:1, bass.ds(e, 1)], min_val=0, max_val=XROWS - 128)
                sp.dma_start(x_rows[bass.ds(first, 128), :], pad[:, :]).then_inc(t_padded, 16)
            sp.wait_ge(t_tab, 2)
            for kind in range(2):
                sp.dma_start(table_dram[kind, :].rearrange("(p g) -> p g", p=128),
                             tab[:, kind, :]).then_inc(t_store, 16)
            sp.wait_ge(t_store, 32)
            sp.dma_start(tab_row[:, :], table_dram.rearrange("(o k) n -> o (k n)", o=1)).then_inc(t_load, 16)
            sp.wait_ge(t_load, 16)
            sp.wait_ge(t_padded, 16 * (E + 1))
            for u in range(2):
                sp.wait_ge(sent[u], 64 * (B // 2))

            def load_tile(t, j, u):
                need(sp, xT_p, t - 3)
                need(sp, didx_d, t - 3)
                first = sp.value_load(tab_row[0:1, bass.ds(t, 1)], min_val=0, max_val=XROWS - 128)
                sp.dma_start(xin[:, u, :], x_rows[bass.ds(first, 128), :]).then_inc(xin_in[u], 16)

            for t in range(4):
                load_tile(t, 0, t)
            with sp.Fori(1, TILES // 4) as j:
                for u in range(4):
                    load_tile(4 * j + u, j, u)

            for u in range(4):
                sp.wait_ge(y_sent[u], 16 * (TILES // 4))
            yv = y_rows.rearrange("(n k) d -> n (k d)", k=TOPK)
            outv = out.rearrange("b t d -> (b t) d")

            def load_y(n, u):
                need(sp, acc_d, TOPK * (n - 3))
                sp.dma_start(yld[:, u, :, :].rearrange("p k d -> p (k d)"),
                             yv[bass.ds(n * T, T), :]).then_inc(yld_in[u], 16)

            def store(n, u):
                need(sp, acc_d, TOPK * (n + 1))
                sp.dma_start(outv[bass.ds(n * T, T), :], acc[:, u, 0, :]).then_inc(out_sent[u], 16)

            for n in range(4):
                load_y(n, n)
            with sp.Fori(0, B // 4 - 1) as j:
                for u in range(4):
                    store(4 * j + u, u)
                    load_y(4 * j + u + 4, u)
            for u in range(4):
                store(B - 4 + u, u)
            for u in range(4):
                sp.wait_ge(out_sent[u], 16 * (B // 4))

        @block.gpsimd
        def _(pool):
            nc.gpsimd.memset(v9[:, :, :, :], 1.0).then_inc(s_v1, 1)
            pool.wait_ge(s_cst, 16)
            nc.gpsimd.tensor_copy(dest[:, 1, :], cst[:, C_DEST:C_DEST + TOPK]).then_inc(s_dest0, 1)
            nc.gpsimd.memset(pad[:, 0:D], 0.0).then_inc(s_pad, 1)
            pool.wait_ge(s_pad, 1)
            nc.gpsimd.tensor_copy(pad[:, D:ROW].bitcast(U32), cst[:, C_PADD:C_PADD + 1]).then_inc(s_pad, 2)

            pool.wait_ge(s_b2g, 1)
            pool.wait_ge(s_dest0, 1)

            def step(i, u, has):
                if has(0):
                    need(pool, xn_d, i + 1)
                    xi = x_all[:, bass.ds(i * D, D)]
                    nc.gpsimd.tensor_tensor(xi, xi, bias2[:, :], ALU.add).then_inc(xb_d, 1)
                if has(-3):
                    m, v = i - 3, 1 - u
                    need(pool, slot_d, m + 1)
                    need_first(pool, dest_d, m)
                    nc.gpsimd.tensor_copy(payload[:, v, :, D:ROW].rearrange("p k o -> p (k o)").bitcast(U32),
                                          dest[:, 1 - v, :]).then_inc(pidx_d, 1)
                    nc.gpsimd.tensor_scalar(dest[:, v, :], dest[:, 1 - v, :], float(T * TOPK), None,
                                            ALU.add).then_inc(dest_d, 1)
                    need_first(pool, pidx_d, m + 1)
                    for k in range(TOPK):
                        nc.gpsimd.indirect_dma_start(
                            x_rows, bass.IndirectOffsetOnAxis(ap=slot[:, v, k:k + 1], axis=0),
                            payload[:, v, k, :], None).then_inc(sent[v], 16)

            pipeline(pool, step)

            def scatter(t, u):
                need(pool, y_d, t + 1)
                need_first(pool, didx_d, t + 1)
                nc.gpsimd.indirect_dma_start(
                    y_rows, bass.IndirectOffsetOnAxis(ap=didx[:, u:u + 1], axis=0), y_sb[:, u, :], None,
                    bounds_check=TOKENS * TOPK - 1, oob_is_err=False).then_inc(y_sent[u], 16)

            with pool.Fori(0, TILES // 4) as j:
                for u in range(4):
                    scatter(4 * j + u, u)

        @block.scalar
        def _(act):
            act.wait_ge(s_vec, 16)
            nc.scalar.activation(tg[:, :], vec[:, V_GX:V_GF + 1], ACT.Tanh).then_inc(s_tg, 1)
            nc.scalar.mul(bq_s[:, :], vec[:, V_BQ:V_BQ + 1], HD ** -0.5).then_inc(s_bq, 1)
            nc.scalar.preload_act_table_set("natural_log_exp_and_others")
            act.wait_ge(s_bq, 1)
            act.wait_ge(s_eps, 1)
            act.wait_ge(s_v1, 1)

            def step(i, u, has):
                o = 1 - u
                if has(2):
                    m = i + 2
                    need(act, mv1_d, m + 1)
                    need(act, xn_d, m - 1)
                    nc.scalar.activation(lv1[:, u:u + 1], mv1[:, u, 1:2], ACT.Ln, bias=eps[:, :]).then_inc(lv1_d, 1)
                    need(act, lv1_d, m + 1)
                    nc.scalar.activation(rs1[:, u:u + 1], lv1[:, u:u + 1], ACT.Exp, scale=-0.5).then_inc(rs1_d, 1)
                if has(1):
                    m = i + 1
                    need(act, k_p, m + 1)
                    if isinstance(m, int):
                        need(act, kbd_in[o], 256 * ((m - o) // 2))
                    else:
                        need(act, kbd_in[o], 128 * (m - o))
                    nc.scalar.activation(kT[:, o, :], ps_f[:, 0:NKV], ACT.Identity,
                                         bias=vec[:, V_BK:V_BK + 1]).then_inc(k_d, 1)
                    need(act, xnT_p, m + 1)
                    need(act, q_p, m - 1)
                    nc.scalar.copy(xnT[:, o, :], ps_f[:, 0:T]).then_inc(xnT_d, 1)
                if has(-2):
                    need(act, oT_p, i - 1)
                    need(act, y_p, i - 2)
                    nc.scalar.copy(oT[:, :], ps_b[:, 0:T]).then_inc(oT_d, 1)

                def group(g):
                    need(act, pt_p, PG * (i - 1) + g + 1)
                    need(act, pv_p, PG * (i - 2) + g + 1)
                    nc.scalar.copy(pT[:, g, :, :].rearrange("p a b -> p (a b)"),
                                   ps_p[g % 2][0:NKV, :]).then_inc(pt_d, 1)

                if has(-1):
                    group(0)
                    group(1)
                if has(1):
                    need(act, q_p, i + 2)
                    need(act, s_p, i)
                    nc.scalar.activation(qT[:, o, :], ps_f[:, 0:T], ACT.Identity, bias=bq_s[:, :],
                                         scale=HD ** -0.5).then_inc(q_d, 1)
                if has(-1):
                    group(2)
                if has(-2):
                    need(act, mv2_d, i - 1)
                    need(act, x2_d, i - 2)
                    nc.scalar.activation(lv2[:, :], mv2[:, 1:2], ACT.Ln, bias=eps[:, :]).then_inc(lv2_d, 1)
                    need(act, lv2_d, i - 1)
                    nc.scalar.activation(rs2[:, :], lv2[:, :], ACT.Exp, scale=-0.5).then_inc(rs2_d, 1)
                if has(-1):
                    group(3)
                if has(1):
                    need(act, v_p, i + 2)
                    need(act, pv_p, PG * i)
                    nc.scalar.copy(v9[:, o, :, 0:HD],
                                   ps_f[0:NKV, 0:D].rearrange("p (h d) -> p h d", d=HD)).then_inc(v_d, 1)
                if has(-3):
                    need(act, ntop_d, i - 2)
                    need(act, gate_d, i - 3)
                    nc.scalar.activation(e4[:, :], top[:, 0:TOPK], ACT.Exp, bias=ntop[:, :],
                                         accum_out=se4[:, :]).then_inc(e4_d, 1)
                if has(0):
                    need(act, diff_d, i + 1)
                    p = prob[:, u, :, :].rearrange("p h k -> p (h k)")
                    nc.scalar.activation(p, p, ACT.Relu, scale=-1.0).then_inc(relu_d, 1)
                    need(act, relu_d, i + 1)
                    nc.scalar.activation(p, p, ACT.Exp, scale=-1.0).then_inc(exp_d, 1)
                if has(-2):
                    need(act, x2T_p, i - 1)
                    need(act, lg_p, i - 2)
                    nc.scalar.copy(x2T[:, :], ps_b[:, 0:T]).then_inc(x2T_d, 1)
                    nc.scalar.copy(x2T_all[:, bass.ds((i - 2) * T, T)], ps_b[:, 0:T]).then_inc(x2Ta_d, 1)

            pipeline(act, step)

            nc.scalar.preload_act_table(ACT.Silu)

            def evac(t, u):
                need(act, xT_p, t + 1)
                need(act, gu_p, t - 1)
                nc.scalar.copy(xT[:, u % 2, :], bank[u % 2][:, 0:128]).then_inc(xT_d, 1)

            def silu(t, u):
                need(act, gu_p, t + 1)
                need(act, h_d, t - 1)
                nc.scalar.activation(sg[:, u % 2, :], bank[2 + u % 2][:, 0:H], ACT.Silu).then_inc(sg_d, 1)

            def y_out(t, u, j=None):
                need(act, dn_p, t + 1)
                if not isinstance(t, int) or t >= 4:
                    act.wait_ge(y_sent[u], 4 * (t - u))
                nc.scalar.copy(y_sb[:, u, :], bank[6 + u % 2][:, 0:D]).then_inc(y_d, 1)

            def tile(t, u, first=False, last=False):
                if not last:
                    evac(t + 1, (u + 1) % 4)
                silu(t, u)
                if not first:
                    y_out(t - 2, (u - 2) % 4)

            evac(0, 0)
            for t in range(4):
                tile(t, t, first=t < 2)
            with act.Fori(1, TILES // 4 - 1) as j:
                for u in range(4):
                    tile(4 * j + u, u)
            for t in range(TILES - 4, TILES):
                tile(t, t % 4, last=t == TILES - 1)
            for t in range(TILES - 2, TILES):
                y_out(t, t % 4)

            def ssilu(n, u):
                need(act, sg_p, 2 * n + 1)
                need(act, hs_d, n - 1)
                nc.scalar.activation(ssg[:, u % 2, :], bank[u % 2][:, :], ACT.Silu).then_inc(ssg_d, 1)

            for n in range(4):
                ssilu(n, n)
            with act.Fori(1, B // 4) as j:
                for u in range(4):
                    ssilu(4 * j + u, u)

        @block.vector
        def _(dve):
            nc.vector.memzero(kbd[:, :, :, :]).then_inc(s_zero, 1)
            nc.vector.memset(eps[:, :], EPS).then_inc(s_eps, 1)
            dve.wait_ge(s_cst, 16)
            nc.vector.tensor_copy(tri[:, :], cst[:, C_TRI:C_TRI + 128]).then_inc(s_tri, 1)
            nc.vector.tensor_copy(ones[:, :], cst[:, C_ONE:C_ONE + 128]).then_inc(s_tri, 1)
            nc.vector.tensor_copy(base[:, 0, :], cst[:, C_EOFF:C_EOFF + E]).then_inc(s_base0, 1)
            dve.wait_ge(s_vec, 16)
            dve.wait_ge(s_bvo, 1)
            nc.vector.tensor_tensor(bias2[:, :], ps_b[:, 0:D], vec[:, V_BO:V_BO + D], ALU.add).then_inc(s_bias, 1)
            dve.wait_ge(s_bias, 1)
            dve.wait_ge(s_tg, 1)
            nc.vector.tensor_scalar(bias2[:, :], bias2[:, :], tg[:, 0:1], None, ALU.mult).then_inc(s_b2g, 1)
            dve.wait_ge(s_base0, 1)
            for q in range(4):
                dve.wait_ge(s_x[q], 16)

            def step(i, u, has):
                o = 1 - u
                if has(-2):
                    m = i - 2
                    ov = ps_o[:, 0:NH * (HD + 1)].rearrange("p (h d) -> p h d", d=HD + 1)
                    need(dve, pv_p, PG * (m + 1))
                    nc.vector.reciprocal(rden[:, :], ov[:, :, HD]).then_inc(rden_d, 1)
                    need(dve, rden_d, m + 1)
                    need(dve, oT_p, m)
                    nc.vector.tensor_tensor(o_sb[:, :].rearrange("p (h d) -> p h d", d=HD), ov[:, :, 0:HD],
                                            rden[:, :].unsqueeze(2).broadcast_to([128, NH, HD]),
                                            ALU.mult).then_inc(on_d, 1)
                if has(-3):
                    m = i - 3
                    need(dve, lg_p, m + 1)
                    nc.vector.tensor_tensor(lg[:, :], ps_b[:, 0:E], vec[:, V_RB:V_RB + E], ALU.add).then_inc(lg_d, 1)
                    need(dve, lg_d, m + 1)
                    need_first(dve, e4_d, m)
                    nc.vector.max(top[:, :], lg[:, :]).then_inc(top_d, 1)
                if has(1):
                    m = i + 1
                    need(dve, rs1_d, m + 1)
                    need(dve, xnT_p, m - 1)
                    nc.vector.tensor_scalar(xn[:, o, :], x_all[:, bass.ds(m * D, D)], mv1[:, o, 0:1],
                                            rs1[:, o:o + 1], ALU.subtract, ALU.mult).then_inc(xn_d, 1)
                if has(-3):
                    m = i - 3
                    need(dve, top_d, m + 1)
                    nc.vector.tensor_scalar(ntop[:, :], top[:, 0:1], -1.0, None, ALU.mult).then_inc(ntop_d, 1)
                    nc.vector.max_index(idx[:, :], top[:, :], lg[:, :]).then_inc(idx_d, 1)
                if has(2):
                    m = i + 2
                    nc.vector.bn_stats(st1[:, u, :], x_all[:, bass.ds(m * D, D)]).then_inc(st1_d, 1)
                if has(-3):
                    m = i - 3
                    need(dve, idx_d, m + 1)
                    nc.vector.tensor_copy(idxf[:, :], idx[:, 0:TOPK]).then_inc(idxf_d, 1)
                if has(2):
                    m = i + 2
                    need_first(dve, st1_d, m + 1)
                    nc.vector.bn_aggr(mv1[:, u, :], st1[:, u, :]).then_inc(mv1_d, 1)
                if has(-3):
                    m = i - 3
                    need(dve, idxf_d, m + 1)
                    need(dve, pre_p, m)
                    nc.vector.tensor_tensor(onehot[:, :, :], iota.unsqueeze(1).broadcast_to([128, TOPK, E]),
                                            idxf[:, :].unsqueeze(2).broadcast_to([128, TOPK, E]),
                                            ALU.is_equal).then_inc(oh_d, 1)
                if has(0):
                    need(dve, s_p, i + 1)
                    for n, (h0, h1) in enumerate(BANKS_S):
                        r = nc.vector.reduce_max(mx[:, h0:h1], ps_s[n][:, 0:(h1 - h0) * NKV].rearrange(
                            "p (h k) -> p h k", k=NKV), AX_X)
                    r.then_inc(mx_d, 1)
                    need(dve, mx_d, i + 1)
                    nc.vector.tensor_scalar(mxc[:, :], mx[:, :], -CLAMP, CLAMP, ALU.max, ALU.min).then_inc(mxc_d, 1)
                if has(-2):
                    m = i - 2
                    need(dve, y_p, m + 1)
                    need(dve, xb_d, m + 1)
                    xi = x_all[:, bass.ds(m * D, D)]
                    nc.vector.scalar_tensor_tensor(out=xi, in0=ps_b[:, 0:D], scalar=tg[:, 0:1], in1=xi,
                                                   op0=ALU.mult, op1=ALU.add).then_inc(x1_d, 1)
                if has(0):
                    need(dve, mxc_d, i + 1)
                    need(dve, pt_p, PG * (i - 1))
                    for n, (h0, h1) in enumerate(BANKS_S):
                        if n == 1 and has(-2):
                            need_first(dve, x1_d, i - 1)
                            nc.vector.bn_stats(st2[:, :], xi).then_inc(st2_d, 1)
                        if n == 2 and has(-2):
                            need_first(dve, st2_d, i - 1)
                            nc.vector.bn_aggr(mv2[:, :], st2[:, :]).then_inc(mv2_d, 1)
                        r = nc.vector.scalar_tensor_tensor(
                            out=prob[:, u, h0:h1, :],
                            in0=ps_s[n][:, 0:(h1 - h0) * NKV].rearrange("p (h k) -> p h k", k=NKV), scalar=-CLAMP,
                            in1=mxc[:, h0:h1].unsqueeze(2).broadcast_to([128, h1 - h0, NKV]),
                            op0=ALU.max, op1=ALU.subtract)
                    r.then_inc(diff_d, 1)
                elif has(-2):
                    need(dve, x1_d, i - 1)
                    nc.vector.bn_stats(st2[:, :], xi).then_inc(st2_d, 1)
                    need(dve, st2_d, i - 1)
                    nc.vector.bn_aggr(mv2[:, :], st2[:, :]).then_inc(mv2_d, 1)
                if has(-3):
                    m, v = i - 3, o
                    need(dve, pre_p, m + 1)
                    need(dve, base_d, m)
                    nc.vector.tensor_tensor(pos[:, :], ps_b[:, 0:E], base[:, v, :], ALU.add).then_inc(pos_d, 1)
                    nc.vector.tensor_tensor(base[:, 1 - v, :], ps_b[:, E:2 * E], base[:, v, :],
                                            ALU.add).then_inc(base_d, 1)
                    need(dve, pos_d, m + 1)
                    nc.vector.tensor_tensor(prod[:, :, :], onehot[:, :, :],
                                            pos[:, :].unsqueeze(1).broadcast_to([128, TOPK, E]),
                                            ALU.mult).then_inc(prod_d, 1)
                if has(-2):
                    m = i - 2
                    need(dve, rs2_d, m + 1)
                    if isinstance(m, int):
                        need(dve, sent[u], 64 * ((m - u) // 2))
                    else:
                        need(dve, sent[u], 32 * (m - u))
                    nc.vector.tensor_scalar(payload[:, u, :, 0:D], xi.unsqueeze(1).broadcast_to([128, TOPK, D]),
                                            mv2[:, 0:1], rs2[:, :], ALU.subtract, ALU.mult).then_inc(x2_d, 1)
                if has(-3):
                    m, v = i - 3, o
                    need(dve, prod_d, m + 1)
                    nc.vector.reduce_sum(slotf[:, :], prod[:, :, :], AX_X).then_inc(slotf_d, 1)
                    need(dve, e4_d, m + 1)
                    nc.vector.reciprocal(rse4[:, :], se4[:, :]).then_inc(rse_d, 1)
                    need(dve, slotf_d, m + 1)
                    nc.vector.tensor_copy(slot[:, v, :], slotf[:, :]).then_inc(slot_d, 1)
                    need(dve, rse_d, m + 1)
                    nc.vector.tensor_scalar(gates[:, bass.ds(m * TOPK, TOPK)], e4[:, :], rse4[:, :], tg[:, 1:2],
                                            ALU.mult, ALU.mult).then_inc(gate_d, 1)

            pipeline(dve, step)

            steps = [0]

            def link(ins):
                steps[0] += 1
                ins.then_inc(t_step, 1)
                dve.wait_ge(t_step, steps[0])

            last = base[:, B % 2, :]
            dve.wait_ge(base_d, B)
            nc.vector.tensor_copy(basei[:, :], base[0:1, B % 2, :]).then_inc(t_basei, 1)
            link(nc.vector.tensor_tensor(cnt[:, :], last, cst[:, C_EOFF:C_EOFF + E], ALU.subtract))
            link(nc.vector.tensor_tensor(cmpj[:, :, :], cnt[:, :].unsqueeze(2).broadcast_to([128, E, 64]),
                                         cst[:, C_J128:C_J128 + 64].unsqueeze(1).broadcast_to([128, E, 64]),
                                         ALU.is_gt))
            link(nc.vector.reduce_sum(ntile[:, :], cmpj[:, :, :], AX_X))
            link(nc.vector.tensor_tensor(lowp[:, :, :], ntile[:, :].unsqueeze(1).broadcast_to([128, E, E]),
                                         cst[:, C_LOW:C_LOW + E * E].rearrange("p (a b) -> p a b", b=E), ALU.mult))
            link(nc.vector.reduce_sum(ends[:, :], lowp[:, :, :], AX_X))
            link(nc.vector.tensor_tensor(starts[:, :], ends[:, :], ntile[:, :], ALU.subtract))
            link(nc.vector.scalar_tensor_tensor(out=adj[:, :], in0=starts[:, :], scalar=-128.0,
                                                in1=cst[:, C_EOFF:C_EOFF + E], op0=ALU.mult, op1=ALU.add))
            tnum = cst[:, C_T:C_T + TGROUPS]
            wide = [128, TGROUPS, E]
            link(nc.vector.tensor_tensor(past[:, :, :], tnum.unsqueeze(2).broadcast_to(wide),
                                         ends[:, :].unsqueeze(1).broadcast_to(wide), ALU.is_ge))
            link(nc.vector.reduce_sum(et[:, :], past[:, :, :], AX_X))
            link(nc.vector.tensor_scalar(valid[:, :], et[:, :], float(E), None, ALU.is_lt))
            link(nc.vector.tensor_tensor(oht[:, :, :], iota.unsqueeze(1).broadcast_to(wide),
                                         et[:, :].unsqueeze(2).broadcast_to(wide), ALU.is_equal))
            link(nc.vector.tensor_tensor(past[:, :, :], oht[:, :, :],
                                         adj[:, :].unsqueeze(1).broadcast_to(wide), ALU.mult))
            link(nc.vector.reduce_sum(srow[:, :], past[:, :, :], AX_X))
            link(nc.vector.tensor_scalar(trow[:, :], tnum, 128.0, float(-DUMMY), ALU.mult, ALU.add))
            link(nc.vector.tensor_tensor(row2[:, :], trow[:, :], valid[:, :], ALU.mult))
            link(nc.vector.tensor_tensor(trow[:, :], row2[:, :], srow[:, :], ALU.add))
            nc.vector.tensor_scalar(tab[:, 0, :], trow[:, :], float(DUMMY), None, ALU.add).then_inc(t_tab, 1)
            nc.vector.tensor_scalar(tab[:, 1, :], et[:, :], float(E - 1), None, ALU.min).then_inc(t_tab, 1)

            def hidden(t, u):
                need(dve, sg_d, t + 1)
                need(dve, hT_p, t - 1)
                nc.vector.tensor_tensor(h[:, u % 2, :], sg[:, u % 2, :], bank[2 + u % 2][:, H:2 * H],
                                        ALU.mult).then_inc(h_d, 1)

            def take_dest(t, u):
                if isinstance(t, int):
                    need(dve, xin_in[u], 16 * ((t - u) // 4 + 1))
                    need(dve, y_sent[u], 16 * ((t - u) // 4))
                else:
                    need(dve, xin_in[u], 4 * (t - u) + 16)
                    need(dve, y_sent[u], 4 * (t - u))
                nc.vector.tensor_copy(didx[:, u:u + 1], xin[:, u, D:ROW].bitcast(U32)).then_inc(didx_d, 1)

            def h_turned(t, u):
                need(dve, hT_p, t + 1)
                need(dve, dn_p, t - 1)
                nc.vector.tensor_copy(hT[:, u % 2, :], bank[4 + u % 2][:, 0:128]).then_inc(hT_d, 1)

            def tile(t, u, first=False):
                hidden(t, u)
                take_dest(t, u)
                if not first:
                    h_turned(t - 1, (u - 1) % 4)

            for t in range(4):
                tile(t, t, first=t == 0)
            with dve.Fori(1, TILES // 4) as j:
                for u in range(4):
                    tile(4 * j + u, u)
            h_turned(TILES - 1, 3)

            def shared_hidden(n, u):
                need(dve, ssg_d, n + 1)
                need(dve, sg_p, 2 * n + 2)
                need(dve, sy_p, 4 * (n - 1))
                nc.vector.tensor_tensor(hs[:, u % 2, :], ssg[:, u % 2, :], bank[2 + u % 2][:, :],
                                        ALU.mult).then_inc(hs_d, 1)

            def take(n, q):
                need(dve, sy_p, 4 * (n - q) + 12 + q + 1)
                if isinstance(n, int):
                    need(dve, out_sent[q], 16 * ((n - q) // 4))
                else:
                    need(dve, out_sent[q], 4 * (n - q))
                nc.vector.scalar_tensor_tensor(out=acc[:, q, 0, :], in0=bank[4 + q][:, 0:D], scalar=tg[:, 1:2],
                                               in1=x_all[:, bass.ds(n * D, D)], op0=ALU.mult,
                                               op1=ALU.add).then_inc(take_d, 1)

            def combine(n, q):
                if isinstance(n, int):
                    need(dve, yld_in[q], 16 * ((n - q) // 4 + 1))
                else:
                    need(dve, yld_in[q], 4 * (n - q) + 16)
                need(dve, take_d, n + 1)
                for k in range(TOPK):
                    if k:
                        need(dve, acc_d, TOPK * n + k)
                    nc.vector.scalar_tensor_tensor(out=acc[:, q, (k + 1) % 2, :], in0=yld[:, q, k, :],
                                                   scalar=gates[:, bass.ds(n * TOPK + k, 1)],
                                                   in1=acc[:, q, k % 2, :], op0=ALU.mult,
                                                   op1=ALU.add).then_inc(acc_d, 1)

            for n in range(4):
                shared_hidden(n, n)
            for u in range(4):
                dve.wait_ge(yld_in[u], 16)
            with dve.Fori(1, B // 4) as c:
                for u in range(4):
                    shared_hidden(4 * c + u, u)
                    if u == 0:
                        for q in range(4):
                            take(4 * c + q - 4, q)
                    combine(4 * c + u - 4, u)
            for q in range(4):
                take(B - 4 + q, q)
            for q in range(4):
                combine(B - 4 + q, q)

        @block.tensor
        def _(pe):
            pe.wait_ge(s_cst, 16)
            pe.wait_ge(s_w, 16)
            pe.wait_ge(s_wkv, 32)
            pe.wait_ge(s_vec, 16)
            nc.tensor.matmul(ps_b[:, 0:D], vec[:, V_BV:V_BV + D], w[:, W_O:W_O + D], start=True,
                             stop=True).then_inc(s_bvo, 1)
            pe.wait_ge(s_tri, 2)
            pe.wait_ge(s_b2g, 1)

            def step(i, u, has):
                o = 1 - u
                if has(0):
                    need(pe, q_d, i + 1)
                    if isinstance(i, int):
                        need(pe, kbd_in[u], 256 * ((i - u) // 2 + 1))
                    else:
                        need(pe, kbd_in[u], 128 * (i - u) + 256)
                    need(pe, diff_d, i)
                for n, (h0, h1) in enumerate(BANKS_S):
                    if n == 1 and has(-3):
                        need(pe, x2T_d, i - 2)
                        need(pe, x2Ta_d, i - 2)
                        nc.tensor.matmul(ps_b[:, 0:E], x2T[:, :], w[:, W_R:W_R + E], start=True,
                                         stop=True).then_inc(lg_p, 1)
                    if has(0):
                        r = nc.tensor.matmul(ps_s[n][:, 0:(h1 - h0) * NKV], qT[:, u, :],
                                             kbd[:, u, h0:h1, :].rearrange("p h k -> p (h k)"), start=True, stop=True)
                if has(0):
                    r.then_inc(s_p, 1)
                if has(1):
                    m = i + 1
                    if isinstance(m, int):
                        need(pe, ctx_in[o], 16 * ((m - o) // 2 + 1))
                    else:
                        need(pe, ctx_in[o], 8 * (m - o) + 16)
                    need(pe, v_d, m)
                    nc.tensor.matmul(ps_f[:, 0:NKV], wk_sb[:, :], ctx_sb[:, o, :], start=True,
                                     stop=True).then_inc(k_p, 1)
                if has(-2):
                    m = i - 2
                    need(pe, on_d, m + 1)
                    need(pe, lg_d, m)
                    need(pe, x2Ta_d, m)
                    nc.tensor.transpose(ps_b[:, 0:T], o_sb[:, :], ident).then_inc(oT_p, 1)
                if has(1):
                    need(pe, k_d, i + 2)
                    need(pe, xn_d, i + 2)
                    nc.tensor.transpose(ps_f[:, 0:T], xn[:, o, :], ident).then_inc(xnT_p, 1)

                def turn(g):
                    m = i - 1
                    need(pe, exp_d, m + 1)
                    need(pe, pt_d, PG * m + g - 1)
                    for a in range(4):
                        r = nc.tensor.transpose(ps_p[g % 2][0:NKV, a * T:(a + 1) * T], prob[:, o, 4 * g + a, :],
                                                ident)
                    r.then_inc(pt_p, 1)

                def context(g):
                    m = i - 1
                    need(pe, pt_d, PG * m + g + 1)
                    if g == 0:
                        need(pe, v_d, m + 1)
                        need(pe, on_d, m)
                    for a in range(4):
                        hh = 4 * g + a
                        r = nc.tensor.matmul(ps_o[:, hh * (HD + 1):(hh + 1) * (HD + 1)], pT[:, g, a, :],
                                             v9[:, o, hh, :], start=True, stop=True)
                    r.then_inc(pv_p, 1)

                if has(-1):
                    turn(0)
                    turn(1)
                if has(1):
                    need(pe, xnT_d, i + 2)
                    nc.tensor.matmul(ps_f[:, 0:T], w[:, W_Q:W_Q + D], xnT[:, o, :], start=True,
                                     stop=True).then_inc(q_p, 1)
                if has(-2):
                    need(pe, oT_d, i - 1)
                    nc.tensor.matmul(ps_b[:, 0:D], oT[:, :], w[:, W_O:W_O + D], start=True, stop=True).then_inc(y_p, 1)
                if has(-1):
                    context(0)
                    turn(2)
                if has(1):
                    need(pe, q_d, i + 2)
                    nc.tensor.matmul(ps_f[0:NKV, 0:D], ctx_sb[:, o, :], wv_sb[:, :], start=True,
                                     stop=True).then_inc(v_p, 1)
                if has(-1):
                    context(1)
                    turn(3)
                if has(-3):
                    m = i - 3
                    need(pe, oh_d, m + 1)
                    need(pe, x1_d, m + 2 if has(-2) else 0)
                    for n, lhs in enumerate((tri, ones)):
                        for k in range(TOPK):
                            r = nc.tensor.matmul(ps_b[:, n * E:(n + 1) * E], lhs[:, :], onehot[:, k, :],
                                                 start=k == 0, stop=k == TOPK - 1)
                    r.then_inc(pre_p, 1)
                if has(-1):
                    context(2)
                if has(-2):
                    m = i - 2
                    need(pe, x2_d, m + 1)
                    need(pe, x1_d, m + 1)
                    need(pe, base_d, m)
                    nc.tensor.transpose(ps_b[:, 0:T], payload[:, u, 0, 0:D], ident).then_inc(x2T_p, 1)
                if has(-1):
                    context(3)

            pipeline(pe, step)

            pe.wait_ge(s_moe, 32)
            pe.wait_ge(t_load, 16)

            def turn_x(t, u):
                if isinstance(t, int):
                    need(pe, xin_in[u], 16 * ((t - u) // 4 + 1))
                else:
                    need(pe, xin_in[u], 4 * (t - u) + 16)
                need(pe, xT_d, t - 1)
                nc.tensor.transpose(bank[u % 2][:, 0:128], xin[:, u, 0:D], ident).then_inc(xT_p, 1)

            def expert_of(t):
                return pe.value_load(tab_row[0:1, bass.ds(TGROUPS * 128 + t, 1)], min_val=0, max_val=E - 1)

            def gate_up(t, u):
                e = expert_of(t)
                need(pe, xT_d, t + 1)
                need(pe, h_d, t - 1)
                nc.tensor.matmul(bank[2 + u % 2][:, 0:2 * H], xT[:, u % 2, :], w_gu[:, bass.ds(e * (2 * H), 2 * H)],
                                 start=True, stop=True).then_inc(gu_p, 1)

            def turn_h(t, u):
                need(pe, h_d, t + 1)
                need(pe, hT_d, t - 1)
                nc.tensor.transpose(bank[4 + u % 2][:, 0:128], h[:, u % 2, :], ident).then_inc(hT_p, 1)

            def down(t, u):
                e = expert_of(t)
                need(pe, hT_d, t + 1)
                need(pe, y_d, t - 1)
                nc.tensor.matmul(bank[6 + u % 2][:, 0:D], hT[:, u % 2, :], w_dn[:, bass.ds(e * D, D)], start=True,
                                 stop=True).then_inc(dn_p, 1)

            def tile(t, u, n=9, last=False):
                gate_up(t, u)
                if n >= 1:
                    turn_h(t - 1, (u - 1) % 4)
                if not last:
                    turn_x(t + 1, (u + 1) % 4)
                if n >= 2:
                    down(t - 2, (u - 2) % 4)

            turn_x(0, 0)
            for t in range(4):
                tile(t, t, t)
            with pe.Fori(1, TILES // 4 - 1) as j:
                for u in range(4):
                    tile(4 * j + u, u)
            for t in range(TILES - 4, TILES):
                tile(t, t % 4, last=t == TILES - 1)
            turn_h(TILES - 1, 3)
            down(TILES - 2, 2)
            down(TILES - 1, 3)

            pe.wait_ge(sg_d, TILES)
            pe.wait_ge(h_d, TILES)
            pe.wait_ge(xT_d, TILES)
            pe.wait_ge(hT_d, TILES)
            pe.wait_ge(y_d, TILES)
            pe.wait_ge(x2Ta_d, B)

            def shared_up(c, n, u):
                need(pe, ssg_d, n - 1)
                need(pe, hs_d, n - 1)
                for which, (at, bk) in enumerate(((W_SG, u % 2), (W_SU, 2 + u % 2))):
                    nc.tensor.matmul(bank[bk][:, :], w[:, at + 128 * u:at + 128 * (u + 1)],
                                     x2T_all[:, bass.ds(c * 512, 512)], start=True, stop=True).then_inc(sg_p, 1)

            def shared_down(n, u):
                need(pe, hs_d, n + 1)
                for q in range(4):
                    if u == 0:
                        need(pe, take_d, n - 4 + q + 1)
                    nc.tensor.matmul(bank[4 + q][:, 0:D], hs[:, u % 2, q * 128:(q + 1) * 128],
                                     w[:, W_SD + 128 * u:W_SD + 128 * (u + 1)], start=u == 0,
                                     stop=u == NS - 1).then_inc(sy_p, 1)

            shared_up(0, 0, 0)
            for u in range(1, 4):
                shared_up(0, u, u)
                shared_down(u - 1, u - 1)
            with pe.Fori(1, B // 4) as c:
                for u in range(4):
                    shared_up(c, 4 * c + u, u)
                    shared_down(4 * c + u - 1, (u - 1) % 4)
            shared_down(B - 1, 3)


def kernel(**inp):
    import numpy as np
    import concourse.bacc as bacc
    from concourse.bass_utils import run_bass_kernel_spmd as run

    def arr(name):
        return np.asarray(inp[name])

    def rep(v):
        return np.broadcast_to(v, (128, v.size))

    p = np.arange(128)
    f = np.float32
    consts = np.zeros((128, C_END), f)
    consts[:, C_ID:C_ID + 128] = np.eye(128, dtype=f)
    consts[:, C_TRI:C_TRI + 128] = (p[:, None] < p[None, :])
    consts[:, C_ONE:C_ONE + 128] = 1
    consts[:, C_IOTA:C_IOTA + E] = np.arange(E)
    consts[:, C_EOFF:C_EOFF + E] = np.arange(E) * STRIDE
    consts[:, C_J128:C_J128 + 64] = np.arange(64) * 128
    consts[:, C_LOW:C_LOW + E * E] = (np.arange(E)[None, :] <= np.arange(E)[:, None]).reshape(1, -1)
    consts[:, C_T:C_T + TGROUPS] = p[:, None] * TGROUPS + np.arange(TGROUPS)
    consts[:, C_DEST:C_DEST + TOPK] = p[:, None] * TOPK + np.arange(TOPK)
    consts[:, C_PADD] = NOWHERE
    sd = arr("L0_ffn_sdown_w").T.reshape(NS, 128, D).transpose(1, 0, 2).reshape(128, HS)
    wts = np.concatenate([arr("L0_xattn_Wq"), arr("L0_xattn_Wo"), arr("L0_ffn_router_w").T,
                          arr("L0_ffn_sgate_w").T, arr("L0_ffn_sup_w").T, sd], axis=1)
    vecs = np.concatenate([rep(arr("L0_ffn_router_bias")), rep(arr("L0_xattn_bo")),
                           rep(arr("L0_xattn_bv")).T, arr("L0_xattn_bq")[:, None], arr("L0_xattn_bk")[:, None],
                           rep(arr("g_xattn")), rep(arr("g_ffn"))], axis=1)
    gu = np.concatenate([arr("L0_ffn_gate_w"), arr("L0_ffn_up_w")], axis=1).transpose(2, 0, 1).reshape(D, E * 2 * H)
    dn = arr("L0_ffn_down_w").transpose(2, 0, 1).reshape(H, E * D)
    ins = {
        "x": arr("x"),
        "ctxT": arr("ctx_768").transpose(2, 0, 1).reshape(CKV, B * NKV),
        "wk": arr("L0_xattn_Wk"), "wv": arr("L0_xattn_Wv"),
        "wts": wts, "vecs": vecs, "consts": consts, "gu": gu, "dn": dn,
    }
    ins = {k: np.ascontiguousarray(v) for k, v in ins.items()}
    nc = bacc.Bacc("TRN2", target_bir_lowering=False, num_devices=1)
    aps = [nc.dram_tensor(f"in_{k}", v.shape, mybir.dt.from_np(v.dtype), kind="ExternalInput").ap()
           for k, v in ins.items()]
    out = nc.dram_tensor("out", (B, T, D), F32, kind="ExternalOutput").ap()
    build(nc, *aps, out)
    r = run(nc, [{f"in_{k}": v for k, v in ins.items()}], core_ids=[0])
    return r.results[0]["out"]
```

```python
from contextlib import ExitStack

import concourse.bass as bass
from concourse import mybir

F32 = mybir.dt.float32
BF16 = mybir.dt.bfloat16
U32 = mybir.dt.uint32
I32 = mybir.dt.int32
ALU = mybir.AluOpType
ACT = mybir.ActivationFunctionType
AX_X = mybir.AxisListType.X

B, T, D = 64, 128, 128
NKV, CKV = 77, 96
NH = 16
HD = D // NH
CLAMP = 10000.0
EPS = 1e-5
E, H = 32, 128
TOPK = 4
HS = 512
NS = HS // 128
TOKENS = B * T
ROW = D + 1
STRIDE = TOKENS + 128
DUMMY = E * STRIDE
XROWS = DUMMY + 128
TILES = 288
TG = TILES // 4
PADS_SP = 20
NOWHERE = 1 << 20

C_ID, C_TRI, C_ONE, C_IOTA, C_EOFF, C_T, C_DEST, C_STEP, C_ZERO, C_PADD, C_P, C_MASK, C_IND, C_END = (
    0, 128, 256, 384, 416, 448, 456, 460, 464, 468, 469, 470, 474, 486)
W_Q, W_O, W_R, W_SG, W_SU, W_SD, W_END = 0, 128, 256, 288, 800, 1312, 1824
V_RB, V_BO, V_BQ, V_GX, V_GF, V_END = 0, 32, 160, 161, 162, 163
GH = 4
NG = NH // GH
GK = GH * NKV
CH = -(-GK // 128)
LASTCH = GK - 128 * (CH - 1)
FILLS = NG * CH // 4
GC = GH * HD + GH
GS = 4 * GC
PROBS = NG * GK + 128 * CH - GK


def build(nc, x, ctxT, wk, wv, wts, vecs, consts, gu, dn, out):
    x_rows = nc.dram_tensor("x_rows", (XROWS, ROW), F32).ap()
    y_rows = nc.dram_tensor("y_rows", (TOKENS * TOPK, D), F32).ap()
    row_dram = nc.dram_tensor("row_dram", (TG, 4), I32).ap()
    exp_dram = nc.dram_tensor("exp_dram", (TG, 8), I32).ap()

    with ExitStack() as stack:
        def sb(name, shape, dt=F32):
            return stack.enter_context(nc.sbuf_tensor(name, shape, dt))

        def sem(name):
            return stack.enter_context(nc.semaphore(name))

        def sems(name, n=2):
            return [sem(f"{name}{i}") for i in range(n)]

        cst = sb("cst", [128, C_END])
        w = sb("w", [128, W_END])
        vec = sb("vec", [128, V_END])
        wk_sb = sb("wk_sb", [CKV + 1, D])
        wv_sb = sb("wv_sb", [CKV + 1, D])
        w_gu = sb("w_gu", [128, E * 2 * H])
        w_dn = sb("w_dn", [128, E * D])
        x_all = sb("x_all", [128, B * D])
        x2T_all = sb("x2T_all", [128, TOKENS])
        gates = sb("gates", [128, B * TOPK])
        tg = sb("tg", [128, 2])
        eps = sb("eps", [128, 1])
        bq_s = sb("bq_s", [128, 1])
        bias2 = sb("bias2", [128, D])
        tri = sb("tri", [128, 128], BF16)
        ones = sb("ones", [128, 128], BF16)
        base = sb("base", [128, 2, E])
        ident = cst[:, C_ID:C_ID + 128]
        iota = cst[:, C_IOTA:C_IOTA + E]

        ctx_sb = sb("ctx_sb", [CKV + 1, 2, NKV])
        st1 = sb("st1", [128, 2, 6])
        mv1 = sb("mv1", [128, 2, 2])
        lv1 = sb("lv1", [128, 2])
        rs1 = sb("rs1", [128, 2])
        xc = sb("xc", [128, D])
        xn = sb("xn", [128, 2, D])
        xnT = sb("xnT", [128, 2, T])
        kvbd = sb("kvbd", [128, 2, 2, GH, NKV])
        qT = sb("qT", [128, 2, T])
        vt = sb("vt", [128, 2, CH, NG, GC])
        mx = sb("mx", [128, NH])
        mxc = sb("mxc", [128, NH])
        prob = sb("prob", [128, 2, PROBS])
        pT = sb("pT", [128, FILLS, 4, T])
        rden = sb("rden", [128, NH])
        o_sb = sb("o_sb", [128, D])
        oT = sb("oT", [128, T])
        st2 = sb("st2", [128, 6])
        mv2 = sb("mv2", [128, 2])
        lv2 = sb("lv2", [128, 1])
        rs2 = sb("rs2", [128, 1])
        payload = sb("payload", [128, 2, TOPK, ROW])
        x2T = sb("x2T", [128, T])
        lg = sb("lg", [128, E])
        top = sb("top", [128, 8])
        ntop = sb("ntop", [128, 1])
        idx = sb("idx", [128, 8], U32)
        idxf = sb("idxf", [128, TOPK])
        onehot = sb("onehot", [128, TOPK, E], BF16)
        e4 = sb("e4", [128, TOPK])
        se4 = sb("se4", [128, 1])
        rse4 = sb("rse4", [128, 1])
        pos = sb("pos", [128, E])
        prod = sb("prod", [128, TOPK, E])
        slotf = sb("slotf", [128, TOPK])
        slot = sb("slot", [128, 2, TOPK], U32)
        dest = sb("dest", [128, 2, TOPK])

        cnt = sb("cnt", [128, E])
        cnti = sb("cnti", [128, E], I32)
        ntilei = sb("ntilei", [128, E], I32)
        ntile = sb("ntile", [128, E])
        ends = sb("ends", [128, E])
        starts = sb("starts", [128, E])
        adj = sb("adj", [128, E])
        past = sb("past", [128, 8, E])
        et = sb("et", [128, 8])
        valid = sb("valid", [128, 4])
        oht = sb("oht", [128, 4, E])
        srow = sb("srow", [128, 4])
        trow = sb("trow", [128, 4])
        row2 = sb("row2", [128, 4])
        tab_r = sb("tab_r", [128, 4], I32)
        tab_e = sb("tab_e", [128, 8], I32)
        basei = sb("basei", [1, E], I32)
        padidx = sb("padidx", [128, E], U32)
        rows_sb = sb("rows_sb", [1, TG * 4], I32)
        exps_sb = sb("exps_sb", [1, TG * 8], I32)
        pad = sb("pad", [128, ROW])

        xin = sb("xin", [128, 4, ROW])
        xT = sb("xT", [128, 2, 128])
        sg = sb("sg", [128, 2, H])
        h = sb("h", [128, 2, H])
        hT = sb("hT", [128, 2, 128])
        y_sb = sb("y_sb", [128, 4, D])
        didx = sb("didx", [128, 4], U32)

        ssg = sb("ssg", [128, 2, 512])
        hs = sb("hs", [128, 2, 512])
        yld = w_gu[:, 0:4 * TOPK * D].rearrange("p (q k d) -> p q k d", q=4, k=TOPK)
        acc = w_gu[:, 4 * TOPK * D:4 * (TOPK + 2) * D].rearrange("p (q k d) -> p q k d", q=4, k=2)

        ps = stack.enter_context(nc.psum_tensor("ps", [128, 8, 512], F32))
        bank = [ps[:, i, :] for i in range(8)]
        ps_p, ps_o, ps_f, ps_b = bank[4:8]

        s_cst, s_w, s_vec, s_wkv, s_moe = sem("s_cst"), sem("s_w"), sem("s_vec"), sem("s_wkv"), sem("s_moe")
        s_x = sems("s_x", 4)
        s_zero, s_tg, s_eps, s_bq, s_b2g = (sem(n) for n in ("s_zero", "s_tg", "s_eps", "s_bq", "s_b2g"))
        s_tri, s_base0, s_dest0, s_pad = sem("s_tri"), sem("s_base0"), sem("s_dest0"), sem("s_pad")
        ctx_in, sent = sems("ctx_in"), sems("sent")
        names = ("st1_d mv1_d lv1_d rs1_d xc_d xn_d xnT_p xnT_d kv_p kv_d q_p q_d vt_p vt_d s_p mx_d mxc_d diff_d relu_d "
                 "exp_d pt_p pt_d pv_p rden_d on_d oT_p oT_d y_p xb_d x1_d st2_d mv2_d lv2_d rs2_d x2_d x2T_p x2T_d "
                 "x2Ta_d lg_p lg_d top_d ntop_d idx_d idxf_d oh_d pre_p pos_d base_d prod_d slotf_d slot_d e4_d "
                 "rse_d gate_d pidx_d dest_d")
        S = {n: sem(n) for n in names.split()}
        (st1_d, mv1_d, lv1_d, rs1_d, xc_d, xn_d, xnT_p, xnT_d, kv_p, kv_d, q_p, q_d, vt_p, vt_d, s_p, mx_d, mxc_d, diff_d,
         relu_d, exp_d, pt_p, pt_d, pv_p, rden_d, on_d, oT_p, oT_d, y_p, xb_d, x1_d, st2_d, mv2_d, lv2_d, rs2_d,
         x2_d, x2T_p, x2T_d, x2Ta_d, lg_p, lg_d, top_d, ntop_d, idx_d, idxf_d, oh_d, pre_p, pos_d, base_d, prod_d,
         slotf_d, slot_d, e4_d, rse_d, gate_d, pidx_d, dest_d) = S.values()
        t_step, t_tab, t_store, t_load, t_padded, t_padded2, t_basei, t_padidx = (sem(n) for n in (
            "t_step", "t_tab", "t_store", "t_load", "t_padded", "t_padded2", "t_basei", "t_padidx"))
        xin_in, y_sent = sems("xin_in", 4), sems("y_sent", 4)
        xT_p, xT_d, gu_p, sg_d, h_d, hT_p, hT_d, dn_p, y_d, didx_d = (sem(n) for n in (
            "xT_p", "xT_d", "gu_p", "sg_d", "h_d", "hT_p", "hT_d", "dn_p", "y_d", "didx_d"))
        yld_in, out_sent = sems("yld_in", 4), sems("out_sent", 4)
        sg_p, ssg_d, hs_d, sy_p, take_d, acc_d = (sem(n) for n in ("sg_p", "ssg_d", "hs_d", "sy_p", "take_d", "acc_d"))

        def need(eng, s, count):
            if not isinstance(count, int) or count > 0:
                eng.wait_ge(s, count)

        passed = sem("passed")

        def need_first(eng, s, count):
            need(eng, s, count)
            if not isinstance(count, int):
                eng.sem_inc(passed, 1)

        def pipeline(eng, step):
            for i in range(-2, 6):
                step(i, i % 2, lambda k, i=i: 0 <= i + k < B)
            with eng.Fori(3, B // 2 - 1) as j:
                for u in range(2):
                    step(2 * j + u, u, lambda k: True)
            for i in range(B - 2, B + 3):
                step(i, i % 2, lambda k, i=i: 0 <= i + k < B)

        def upto(m, u, each, slots=2):
            return each * ((m - u) // slots) if isinstance(m, int) else each // slots * (m - u)

        def four(eng, table, j, n, top):
            return nc.values_load_multi_w_load_instructions(
                table[0:1, bass.ds(j * n, n)], engines=[eng.engine], min_val=0, max_val=top,
                                  skip_runtime_bounds_check_because="the table is computed within its bounds")[1]

        block = stack.enter_context(nc.Block())

        @block.sync
        def _(sp):
            sp.dma_start(cst[:, :], consts).then_inc(s_cst, 16)
            sp.dma_start(vec[:, :], vecs).then_inc(s_vec, 16)
            xv = x.rearrange("b t d -> t b d")
            at = 0
            for q, n in enumerate((2, 14, 16, 32)):
                sp.dma_start(x_all[:, at * D:(at + n) * D].rearrange("p (b d) -> p b d", d=D),
                             xv[:, at:at + n, :]).then_inc(s_x[q], 16)
                at += n
                if q == 0:
                    sp.dma_start(wk_sb[:, :], wk).then_inc(s_wkv, 16)
                    sp.dma_start(wv_sb[:, :], wv).then_inc(s_wkv, 16)
                    for m in range(2):
                        sp.dma_start(ctx_sb[:, m, :], ctxT[:, m * NKV:(m + 1) * NKV]).then_inc(ctx_in[m], 16)
                    sp.dma_start(w[:, :], wts).then_inc(s_w, 16)

            def step(i, u, has):
                if has(2) and not (isinstance(i, int) and i < 0):
                    need(sp, kv_p, i + 1)
                    sp.dma_start(ctx_sb[:, u, :], ctxT[:, bass.ds((i + 2) * NKV, NKV)]).then_inc(ctx_in[u], 16)

            sp.dma_start(w_gu[:, :], gu).then_inc(s_moe, 16)
            sp.dma_start(w_dn[:, :], dn).then_inc(s_moe, 16)
            pipeline(sp, step)

            sp.wait_ge(s_pad, 3)
            sp.wait_ge(t_basei, 1)
            sp.dma_start(x_rows[DUMMY:DUMMY + 128, :], pad[:, :]).then_inc(t_padded, 16)
            with sp.Fori(0, PADS_SP) as e:
                first = sp.value_load(basei[0:1, bass.ds(e, 1)], min_val=0, max_val=XROWS - 128)
                sp.dma_start(x_rows[bass.ds(first, 128), :], pad[:, :]).then_inc(t_padded, 16)
            sp.wait_ge(t_tab, 2)
            sp.dma_start(row_dram, tab_r[0:TG, :]).then_inc(t_store, 16)
            sp.dma_start(exp_dram, tab_e[0:TG, :]).then_inc(t_store, 16)
            sp.wait_ge(t_store, 32)
            sp.dma_start(rows_sb[:, :], row_dram.rearrange("(o n) k -> o (n k)", o=1)).then_inc(t_load, 16)
            sp.dma_start(exps_sb[:, :], exp_dram.rearrange("(o n) k -> o (n k)", o=1)).then_inc(t_load, 16)
            sp.wait_ge(t_load, 32)
            sp.wait_ge(t_padded, 16 * (PADS_SP + 1))
            sp.wait_ge(t_padded2, 16 * (E - PADS_SP))
            for u in range(2):
                sp.wait_ge(sent[u], 64 * (B // 2))

            def load_tiles(j):
                firsts = four(sp, rows_sb, j, 4, XROWS - 128)
                for u in range(4):
                    t = 4 * j + u
                    need(sp, xT_p, t - 3)
                    need(sp, didx_d, t - 3)
                    sp.dma_start(xin[:, u, :], x_rows[bass.ds(firsts[u], 128), :]).then_inc(xin_in[u], 16)

            load_tiles(0)
            with sp.Fori(1, TG) as j:
                load_tiles(j)

            for u in range(4):
                sp.wait_ge(y_sent[u], 16 * (TILES // 4))
            yv = y_rows.rearrange("(n k) d -> n (k d)", k=TOPK)
            outv = out.rearrange("b t d -> (b t) d")

            def load_y(n, u):
                need(sp, acc_d, TOPK * (n - 3))
                sp.dma_start(yld[:, u, :, :].rearrange("p k d -> p (k d)"),
                             yv[bass.ds(n * T, T), :]).then_inc(yld_in[u], 16)

            def store(n, u):
                need(sp, acc_d, TOPK * (n + 1))
                sp.dma_start(outv[bass.ds(n * T, T), :], acc[:, u, 0, :]).then_inc(out_sent[u], 16)

            for n in range(4):
                load_y(n, n)
            with sp.Fori(0, B // 4 - 1) as j:
                for u in range(4):
                    store(4 * j + u, u)
                    load_y(4 * j + u + 4, u)
            for u in range(4):
                store(B - 4 + u, u)
            for u in range(4):
                sp.wait_ge(out_sent[u], 16 * (B // 4))

        @block.gpsimd
        def _(pool):
            pool.wait_ge(s_cst, 16)
            nc.gpsimd.tensor_copy(dest[:, 1, :], cst[:, C_DEST:C_DEST + TOPK]).then_inc(s_dest0, 1)
            nc.gpsimd.memset(pad[:, 0:D], 0.0).then_inc(s_pad, 1)
            pool.wait_ge(s_pad, 1)
            nc.gpsimd.tensor_copy(pad[:, D:ROW].bitcast(U32), cst[:, C_PADD:C_PADD + 1]).then_inc(s_pad, 2)

            pool.wait_ge(s_b2g, 1)
            pool.wait_ge(s_dest0, 1)

            def step(i, u, has):
                o = 1 - u
                if isinstance(i, int) and i in (-1, 1, 3):
                    for q in {-1: (0,), 1: (1,), 3: (2, 3)}[i]:
                        pool.wait_ge(s_x[q], 16)
                if has(1):
                    m = i + 1
                    need(pool, rs1_d, m + 1)
                    need(pool, xnT_p, m - 1)
                    need_first(pool, xn_d, m)
                    nc.gpsimd.tensor_tensor(xc[:, :], x_all[:, bass.ds(m * D, D)],
                                            mv1[:, o, 0:1].broadcast_to([128, D]), ALU.subtract).then_inc(xc_d, 1)
                    need(pool, xc_d, m + 1)
                    nc.gpsimd.tensor_tensor(xn[:, o, :], xc[:, :], rs1[:, o:o + 1].broadcast_to([128, D]),
                                            ALU.mult).then_inc(xn_d, 1)
                if has(0):
                    need_first(pool, xn_d, i + 1)
                    xi = x_all[:, bass.ds(i * D, D)]
                    nc.gpsimd.tensor_tensor(xi, xi, bias2[:, :], ALU.add).then_inc(xb_d, 1)
                if has(-3):
                    m, v = i - 3, o
                    need(pool, slot_d, m + 1)
                    need_first(pool, dest_d, m)
                    nc.gpsimd.tensor_copy(payload[:, v, :, D:ROW].rearrange("p k o -> p (k o)").bitcast(U32),
                                          dest[:, 1 - v, :]).then_inc(pidx_d, 1)
                    need(pool, pidx_d, m + 1)
                    nc.gpsimd.tensor_tensor(dest[:, v, :], dest[:, 1 - v, :], cst[:, C_STEP:C_STEP + TOPK],
                                            ALU.add).then_inc(dest_d, 1)
                    for k in range(TOPK):
                        nc.gpsimd.indirect_dma_start(
                            x_rows, bass.IndirectOffsetOnAxis(ap=slot[:, v, k:k + 1], axis=0),
                            payload[:, v, k, :], None).then_inc(sent[v], 16)

            pipeline(pool, step)

            pool.wait_ge(t_padidx, 1)
            pool.wait_ge(s_pad, 3)
            for e in range(PADS_SP, E):
                nc.gpsimd.indirect_dma_start(x_rows, bass.IndirectOffsetOnAxis(ap=padidx[:, e:e + 1], axis=0),
                                             pad[:, :], None).then_inc(t_padded2, 16)

            def scatter(t, u):
                need_first(pool, y_d, t + 1)
                nc.gpsimd.indirect_dma_start(
                    y_rows, bass.IndirectOffsetOnAxis(ap=didx[:, u:u + 1], axis=0), y_sb[:, u, :], None,
                    bounds_check=TOKENS * TOPK - 1, oob_is_err=False).then_inc(y_sent[u], 16)

            with pool.Fori(0, TG) as j:
                for u in range(4):
                    scatter(4 * j + u, u)

        @block.scalar
        def _(act):
            act.wait_ge(s_vec, 16)
            nc.scalar.activation(tg[:, :], vec[:, V_GX:V_GF + 1], ACT.Tanh).then_inc(s_tg, 1)
            nc.scalar.mul(bq_s[:, :], vec[:, V_BQ:V_BQ + 1], HD ** -0.5).then_inc(s_bq, 1)
            nc.scalar.preload_act_table_set("natural_log_exp_and_others")
            act.wait_ge(s_bq, 1)
            act.wait_ge(s_eps, 1)

            def step(i, u, has):
                o = 1 - u
                if has(2):
                    m = i + 2
                    need(act, mv1_d, m + 1)
                    need(act, xn_d, m - 1)
                    nc.scalar.activation(lv1[:, u:u + 1], mv1[:, u, 1:2], ACT.Ln, bias=eps[:, :]).then_inc(lv1_d, 1)
                    need(act, lv1_d, m + 1)
                    nc.scalar.activation(rs1[:, u:u + 1], lv1[:, u:u + 1], ACT.Exp, scale=-0.5).then_inc(rs1_d, 1)
                if has(-2):
                    need(act, oT_p, i - 1)
                    need(act, y_p, i - 2)
                    nc.scalar.copy(oT[:, :], ps_b[:, 0:T]).then_inc(oT_d, 1)

                def fill(f):
                    need(act, pt_p, FILLS * (i - 1) + f + 1)
                    need(act, pv_p, FILLS * (i - 2) + f + 1)
                    nc.scalar.copy(pT[:, f, :, :].rearrange("p a b -> p (a b)"), ps_p[:, :]).then_inc(pt_d, 1)

                if has(-1):
                    fill(0)
                    fill(1)
                if has(1):
                    need(act, xnT_p, i + 2)
                    need(act, q_p, i)
                    nc.scalar.copy(xnT[:, o, :], ps_f[:, 0:T]).then_inc(xnT_d, 1)
                if has(-1):
                    fill(2)
                if has(-2):
                    need(act, mv2_d, i - 1)
                    need(act, x2_d, i - 2)
                    nc.scalar.activation(lv2[:, :], mv2[:, 1:2], ACT.Ln, bias=eps[:, :]).then_inc(lv2_d, 1)
                    need(act, lv2_d, i - 1)
                    nc.scalar.activation(rs2[:, :], lv2[:, :], ACT.Exp, scale=-0.5).then_inc(rs2_d, 1)
                if has(1):
                    need(act, q_p, i + 2)
                    need(act, s_p, i)
                    nc.scalar.activation(qT[:, o, :], ps_f[:, 0:T], ACT.Identity, bias=bq_s[:, :],
                                         scale=HD ** -0.5).then_inc(q_d, 1)
                if has(-3):
                    need(act, ntop_d, i - 2)
                    need(act, gate_d, i - 3)
                    nc.scalar.activation(e4[:, :], top[:, 0:TOPK], ACT.Exp, bias=ntop[:, :],
                                         accum_out=se4[:, :]).then_inc(e4_d, 1)
                p = prob[:, u, 0:NG * GK]
                if has(0):
                    need(act, diff_d, 2 * (i + 1))
                    nc.scalar.activation(p, p, ACT.Relu, scale=-1.0).then_inc(relu_d, 1)
                if has(1):
                    need(act, vt_p, i + 2)
                    need(act, pv_p, FILLS * i)
                    nc.scalar.copy(vt[:, o, 0:CH - 1, :, 0:GH * HD],
                                   ps_f[:, 0:(CH - 1) * D].rearrange("p (c g d) -> p c g d", c=CH - 1, g=NG)
                                   ).then_inc(vt_d, 1)
                    nc.scalar.copy(vt[0:LASTCH, o, CH - 1, :, 0:GH * HD],
                                   ps_f[0:LASTCH, (CH - 1) * D:CH * D].rearrange("p (g d) -> p g d", g=NG)
                                   ).then_inc(vt_d, 1)
                if has(-2):
                    need(act, x2T_p, i - 1)
                    need(act, lg_p, i - 2)
                    nc.scalar.copy(x2T[:, :], ps_b[:, 0:T]).then_inc(x2T_d, 1)
                    nc.scalar.copy(x2T_all[:, bass.ds((i - 2) * T, T)], ps_b[:, 0:T]).then_inc(x2Ta_d, 1)
                if has(0):
                    need(act, relu_d, i + 1)
                    nc.scalar.activation(p, p, ACT.Exp, scale=-1.0).then_inc(exp_d, 1)

            pipeline(act, step)

            nc.scalar.preload_act_table(ACT.Silu)

            def evac(t, u):
                need(act, xT_p, t + 1)
                need(act, gu_p, t - 1)
                nc.scalar.copy(xT[:, u % 2, :], bank[u % 2][:, 0:128]).then_inc(xT_d, 1)

            def silu(t, u):
                need(act, gu_p, t + 1)
                need(act, h_d, t - 1)
                nc.scalar.activation(sg[:, u % 2, :], bank[2 + u % 2][:, 0:H], ACT.Silu).then_inc(sg_d, 1)

            def h_turned(t, u):
                need(act, hT_p, t + 1)
                need(act, dn_p, t - 1)
                nc.scalar.copy(hT[:, u % 2, :], bank[4 + u % 2][:, 0:128]).then_inc(hT_d, 1)

            def tile(t, u, first=False, last=False):
                if not last:
                    evac(t + 1, (u + 1) % 4)
                silu(t, u)
                if not first:
                    h_turned(t - 1, (u - 1) % 4)

            evac(0, 0)
            for t in range(4):
                tile(t, t, first=t == 0)
            with act.Fori(1, TG - 1) as j:
                for u in range(4):
                    tile(4 * j + u, u)
            for t in range(TILES - 4, TILES):
                tile(t, t % 4, last=t == TILES - 1)
            h_turned(TILES - 1, 3)

            def ssilu(n, u):
                need(act, sg_p, 2 * n + 1)
                need(act, hs_d, n - 1)
                nc.scalar.activation(ssg[:, u % 2, :], bank[u % 2][:, :], ACT.Silu).then_inc(ssg_d, 1)

            for n in range(4):
                ssilu(n, n)
            with act.Fori(1, B // 4) as j:
                for u in range(4):
                    ssilu(4 * j + u, u)

        @block.vector
        def _(dve):
            nc.vector.memset(prob[:, :, NG * GK:PROBS], 0.0).then_inc(s_zero, 1)
            nc.vector.memzero(vt[:, :, :, :, :]).then_inc(s_zero, 1)
            nc.vector.memset(eps[:, :], EPS).then_inc(s_eps, 1)
            dve.wait_ge(s_cst, 16)
            nc.vector.tensor_copy(tri[:, :], cst[:, C_TRI:C_TRI + 128]).then_inc(s_tri, 1)
            nc.vector.tensor_copy(ones[:, :], cst[:, C_ONE:C_ONE + 128]).then_inc(s_tri, 1)
            nc.vector.tensor_copy(base[:, 0, :], cst[:, C_EOFF:C_EOFF + E]).then_inc(s_base0, 1)
            dve.wait_ge(s_zero, 2)
            for n in range(2):
                for g in range(NG):
                    r = nc.vector.tensor_copy(vt[:, n, :, g, GH * HD:GC],
                                              cst[:, C_IND:C_IND + CH * GH].rearrange("p (c a) -> p c a", c=CH))
            r.then_inc(s_zero, 1)
            dve.wait_ge(s_vec, 16)
            dve.wait_ge(s_tg, 1)
            nc.vector.tensor_scalar(bias2[:, :], vec[:, V_BO:V_BO + D], tg[:, 0:1], None, ALU.mult).then_inc(s_b2g, 1)
            dve.wait_ge(s_base0, 1)
            mask = cst[:, C_MASK:C_MASK + GH].unsqueeze(1).unsqueeze(3).broadcast_to([128, 2, GH, NKV])

            def step(i, u, has):
                o = 1 - u
                if isinstance(i, int) and i in (-2, 0, 2):
                    for q in {-2: (0,), 0: (1,), 2: (2, 3)}[i]:
                        dve.wait_ge(s_x[q], 16)
                if has(-2):
                    m = i - 2
                    ov = ps[:, 5:7, :].rearrange("p b n -> p (b n)")[:, 0:NG * GS].rearrange(
                        "p (g c) -> p g c", c=GS)
                    need(dve, pv_p, FILLS * (m + 1))
                    nc.vector.reciprocal(rden[:, :].rearrange("p (g a) -> p g a", a=GH),
                                         ov[:, :, GH * HD:GC]).then_inc(rden_d, 1)
                if has(2):
                    m = i + 2
                    nc.vector.bn_stats(st1[:, u, :], x_all[:, bass.ds(m * D, D)]).then_inc(st1_d, 1)
                if has(-2):
                    need(dve, rden_d, i - 1)
                    need(dve, oT_p, i - 2)
                    nc.vector.tensor_tensor(
                        o_sb[:, :].rearrange("p (g a d) -> p g a d", a=GH, d=HD),
                        ov[:, :, 0:GH * HD].rearrange("p g (a d) -> p g a d", a=GH),
                        rden[:, :].rearrange("p (g a) -> p g a", a=GH).unsqueeze(3).broadcast_to([128, NG, GH, HD]),
                        ALU.mult).then_inc(on_d, 1)
                if has(2):
                    need(dve, xn_d, i + 1)
                    need_first(dve, st1_d, i + 3)
                    nc.vector.bn_aggr(mv1[:, u, :], st1[:, u, :]).then_inc(mv1_d, 1)
                if has(-3):
                    m = i - 3
                    need(dve, lg_p, m + 1)
                    nc.vector.tensor_tensor(lg[:, :], ps_b[:, 0:E], vec[:, V_RB:V_RB + E], ALU.add).then_inc(lg_d, 1)
                    need(dve, lg_d, m + 1)
                    need_first(dve, e4_d, m)
                    nc.vector.max(top[:, :], lg[:, :]).then_inc(top_d, 1)
                    need(dve, top_d, m + 1)
                    nc.vector.tensor_scalar(ntop[:, :], top[:, 0:1], -1.0, None, ALU.mult).then_inc(ntop_d, 1)
                    nc.vector.max_index(idx[:, :], top[:, :], lg[:, :]).then_inc(idx_d, 1)
                if has(0):
                    for n in range(2):
                        need(dve, s_p, 2 * i + n + 1)
                        if n == 1 and has(-3):
                            need(dve, idx_d, i - 2)
                            nc.vector.tensor_copy(idxf[:, :], idx[:, 0:TOPK]).then_inc(idxf_d, 1)
                        nc.vector.reduce_max(mx[:, 2 * GH * n:2 * GH * (n + 1)].rearrange("p (g a) -> p g a", a=GH),
                                             ps[:, 2 * n:2 * n + 2, 0:GK].rearrange("p g (a k) -> p g a k", k=NKV),
                                             AX_X).then_inc(mx_d, 1)
                elif has(-3):
                    need(dve, idx_d, i - 2)
                    nc.vector.tensor_copy(idxf[:, :], idx[:, 0:TOPK]).then_inc(idxf_d, 1)
                if has(-3):
                    m = i - 3
                    need(dve, idxf_d, m + 1)
                    need(dve, pre_p, m)
                    nc.vector.tensor_tensor(onehot[:, :, :], iota.unsqueeze(1).broadcast_to([128, TOPK, E]),
                                            idxf[:, :].unsqueeze(2).broadcast_to([128, TOPK, E]),
                                            ALU.is_equal).then_inc(oh_d, 1)
                if has(0):
                    need(dve, mx_d, 2 * i + 2)
                    nc.vector.tensor_scalar(mxc[:, :], mx[:, :], -CLAMP, CLAMP, ALU.max, ALU.min).then_inc(mxc_d, 1)
                if has(1):
                    m = i + 1
                    need(dve, kv_p, m + 1)
                    need(dve, vt_p, m - 1)
                    nc.vector.tensor_tensor(
                        kvbd[:, o, :, :, :],
                        ps_f[:, 0:2 * NKV].rearrange("p (n k) -> p n k", n=2).unsqueeze(2).broadcast_to(
                            [128, 2, GH, NKV]), mask, ALU.mult).then_inc(kv_d, 1)
                xi = x_all[:, bass.ds((i - 2) * D, D)] if has(-2) else None
                if has(-2):
                    need(dve, y_p, i - 1)
                    need(dve, xb_d, i - 1)
                    nc.vector.scalar_tensor_tensor(out=xi, in0=ps_b[:, 0:D], scalar=tg[:, 0:1], in1=xi,
                                                   op0=ALU.mult, op1=ALU.add).then_inc(x1_d, 1)

                def difference(n):
                    nc.vector.scalar_tensor_tensor(
                        out=prob[:, u, 2 * n * GK:2 * (n + 1) * GK].rearrange("p (g a k) -> p g a k", g=2, a=GH),
                        in0=ps[:, 2 * n:2 * n + 2, 0:GK].rearrange("p g (a k) -> p g a k", k=NKV), scalar=-CLAMP,
                        in1=mxc[:, 2 * GH * n:2 * GH * (n + 1)].rearrange("p (g a) -> p g a", a=GH).unsqueeze(
                            3).broadcast_to([128, 2, GH, NKV]),
                        op0=ALU.max, op1=ALU.subtract).then_inc(diff_d, 1)

                if has(0):
                    need(dve, mxc_d, i + 1)
                    need(dve, pt_p, FILLS * (i - 1))
                    difference(0)
                if has(-2):
                    need_first(dve, x1_d, i - 1)
                    nc.vector.bn_stats(st2[:, :], xi).then_inc(st2_d, 1)
                if has(-3):
                    m, v = i - 3, o
                    need(dve, pre_p, m + 1)
                    need(dve, base_d, m)
                    nc.vector.tensor_tensor(pos[:, :], ps_b[:, 0:E], base[:, v, :], ALU.add).then_inc(pos_d, 1)
                    nc.vector.tensor_tensor(base[:, 1 - v, :], ps_b[:, E:2 * E], base[:, v, :],
                                            ALU.add).then_inc(base_d, 1)
                if has(-2):
                    need_first(dve, st2_d, i - 1)
                    nc.vector.bn_aggr(mv2[:, :], st2[:, :]).then_inc(mv2_d, 1)
                if has(0):
                    difference(1)
                if has(-3):
                    m, v = i - 3, o
                    need(dve, pos_d, m + 1)
                    nc.vector.tensor_tensor(prod[:, :, :], onehot[:, :, :],
                                            pos[:, :].unsqueeze(1).broadcast_to([128, TOPK, E]),
                                            ALU.mult).then_inc(prod_d, 1)
                if has(-2):
                    m = i - 2
                    need(dve, rs2_d, m + 1)
                    need(dve, sent[u], upto(m, u, 64))
                    nc.vector.tensor_scalar(payload[:, u, :, 0:D], xi.unsqueeze(1).broadcast_to([128, TOPK, D]),
                                            mv2[:, 0:1], rs2[:, :], ALU.subtract, ALU.mult).then_inc(x2_d, 1)
                if has(-3):
                    m, v = i - 3, o
                    need(dve, prod_d, m + 1)
                    nc.vector.reduce_sum(slotf[:, :], prod[:, :, :], AX_X).then_inc(slotf_d, 1)
                    need(dve, e4_d, m + 1)
                    nc.vector.reciprocal(rse4[:, :], se4[:, :]).then_inc(rse_d, 1)
                    need(dve, slotf_d, m + 1)
                    nc.vector.tensor_copy(slot[:, v, :], slotf[:, :]).then_inc(slot_d, 1)
                    need(dve, rse_d, m + 1)
                    nc.vector.tensor_scalar(gates[:, bass.ds(m * TOPK, TOPK)], e4[:, :], rse4[:, :], tg[:, 1:2],
                                            ALU.mult, ALU.mult).then_inc(gate_d, 1)

            pipeline(dve, step)

            steps = [0]

            def link(ins):
                steps[0] += 1
                ins.then_inc(t_step, 1)
                dve.wait_ge(t_step, steps[0])

            last = base[:, B % 2, :]
            dve.wait_ge(base_d, B)
            nc.vector.tensor_copy(basei[:, :], base[0:1, B % 2, :]).then_inc(t_basei, 1)
            nc.vector.tensor_scalar(padidx[:, :], last, cst[:, C_P:C_P + 1], None, ALU.add).then_inc(t_padidx, 1)
            link(nc.vector.tensor_tensor(cnt[:, :], last, cst[:, C_EOFF:C_EOFF + E], ALU.subtract))
            link(nc.vector.tensor_scalar(cnti[:, :], cnt[:, :], 127.0, None, ALU.add))
            link(nc.vector.tensor_single_scalar(ntilei[:, :], cnti[:, :], 7, ALU.logical_shift_right))
            link(nc.vector.tensor_copy(ntile[:, :], ntilei[:, :]))
            link(nc.vector.tensor_tensor_scan(ends[:, :], cst[:, C_ONE:C_ONE + E], ntile[:, :], 0.0,
                                              ALU.mult, ALU.add))
            link(nc.vector.tensor_tensor(starts[:, :], ends[:, :], ntile[:, :], ALU.subtract))
            link(nc.vector.scalar_tensor_tensor(out=adj[:, :], in0=starts[:, :], scalar=-128.0,
                                                in1=cst[:, C_EOFF:C_EOFF + E], op0=ALU.mult, op1=ALU.add))
            tnum = cst[:, C_T:C_T + 8]
            wide = [128, 8, E]
            link(nc.vector.tensor_tensor(past[:, :, :], tnum.unsqueeze(2).broadcast_to(wide),
                                         ends[:, :].unsqueeze(1).broadcast_to(wide), ALU.is_ge))
            link(nc.vector.reduce_sum(et[:, :], past[:, :, :], AX_X))
            nc.vector.tensor_scalar(tab_e[:, :], et[:, :], float(E - 1), None, ALU.min).then_inc(t_tab, 1)
            half = [128, 4, E]
            link(nc.vector.tensor_scalar(valid[:, :], et[:, 0:4], float(E), None, ALU.is_lt))
            link(nc.vector.tensor_tensor(oht[:, :, :], iota.unsqueeze(1).broadcast_to(half),
                                         et[:, 0:4].unsqueeze(2).broadcast_to(half), ALU.is_equal))
            link(nc.vector.tensor_tensor(past[:, 0:4, :], oht[:, :, :],
                                         adj[:, :].unsqueeze(1).broadcast_to(half), ALU.mult))
            link(nc.vector.reduce_sum(srow[:, :], past[:, 0:4, :], AX_X))
            link(nc.vector.tensor_scalar(trow[:, :], tnum[:, 0:4], 128.0, float(-DUMMY), ALU.mult, ALU.add))
            link(nc.vector.tensor_tensor(row2[:, :], trow[:, :], valid[:, :], ALU.mult))
            link(nc.vector.tensor_tensor(trow[:, :], row2[:, :], srow[:, :], ALU.add))
            nc.vector.tensor_scalar(tab_r[:, :], trow[:, :], float(DUMMY), None, ALU.add).then_inc(t_tab, 1)

            def hidden(t, u):
                need(dve, sg_d, t + 1)
                need(dve, hT_p, t - 1)
                nc.vector.tensor_tensor(h[:, u % 2, :], sg[:, u % 2, :], bank[2 + u % 2][:, H:2 * H],
                                        ALU.mult).then_inc(h_d, 1)

            def take_dest(t, u, used):
                need(dve, xin_in[u], used + 16)
                need(dve, y_sent[u], used)
                nc.vector.tensor_copy(didx[:, u:u + 1], xin[:, u, D:ROW].bitcast(U32)).then_inc(didx_d, 1)

            def result(t, u):
                need(dve, dn_p, t + 1)
                nc.vector.tensor_copy(y_sb[:, u, :], bank[6 + u % 2][:, 0:D]).then_inc(y_d, 1)

            def tile(t, u, used, n=9):
                hidden(t, u)
                take_dest(t, u, used)
                if n >= 2:
                    result(t - 2, (u - 2) % 4)

            for t in range(4):
                tile(t, t, 0, t)
            with dve.Fori(1, TG) as j:
                used = dve.snap(16 * j)
                for u in range(4):
                    tile(4 * j + u, u, used)
            for t in (TILES - 2, TILES - 1):
                result(t, t % 4)

            def shared_hidden(n, u):
                need(dve, ssg_d, n + 1)
                need(dve, sg_p, 2 * n + 2)
                need(dve, sy_p, 4 * (n - 1))
                nc.vector.tensor_tensor(hs[:, u % 2, :], ssg[:, u % 2, :], bank[2 + u % 2][:, :],
                                        ALU.mult).then_inc(hs_d, 1)

            def take(n, q):
                need(dve, sy_p, 4 * (n - q) + 12 + q + 1)
                if isinstance(n, int):
                    need(dve, out_sent[q], 16 * ((n - q) // 4))
                else:
                    need(dve, out_sent[q], 4 * (n - q))
                nc.vector.scalar_tensor_tensor(out=acc[:, q, 0, :], in0=bank[4 + q][:, 0:D], scalar=tg[:, 1:2],
                                               in1=x_all[:, bass.ds(n * D, D)], op0=ALU.mult,
                                               op1=ALU.add).then_inc(take_d, 1)

            def combine(n, q):
                if isinstance(n, int):
                    need(dve, yld_in[q], 16 * ((n - q) // 4 + 1))
                else:
                    need(dve, yld_in[q], 4 * (n - q) + 16)
                need(dve, take_d, n + 1)
                for k in range(TOPK):
                    if k:
                        need(dve, acc_d, TOPK * n + k)
                    nc.vector.scalar_tensor_tensor(out=acc[:, q, (k + 1) % 2, :], in0=yld[:, q, k, :],
                                                   scalar=gates[:, bass.ds(n * TOPK + k, 1)],
                                                   in1=acc[:, q, k % 2, :], op0=ALU.mult,
                                                   op1=ALU.add).then_inc(acc_d, 1)

            for n in range(4):
                shared_hidden(n, n)
            for u in range(4):
                dve.wait_ge(yld_in[u], 16)

            def chunk(c):
                for u in range(4):
                    shared_hidden(4 * c + u, u)
                    if u == 0:
                        for q in range(4):
                            take(4 * c + q - 4, q)
                    combine(4 * c + u - 4, u)

            chunk(1)
            with dve.Fori(2, B // 4) as c:
                chunk(c)
            for q in range(4):
                take(B - 4 + q, q)
            for q in range(4):
                combine(B - 4 + q, q)

        @block.tensor
        def _(pe):
            pe.wait_ge(s_cst, 16)
            pe.wait_ge(s_w, 16)
            pe.wait_ge(s_wkv, 32)
            pe.wait_ge(s_vec, 16)
            pe.wait_ge(s_tri, 2)
            pe.wait_ge(s_zero, 3)

            def step(i, u, has):
                o = 1 - u
                if has(0):
                    need(pe, q_d, i + 1)
                    need(pe, kv_d, i + 1)
                    need(pe, diff_d, 2 * i)
                for g in range(NG):
                    if g == 2 and has(-3):
                        need(pe, x2Ta_d, i - 2)
                        nc.tensor.matmul(ps_b[:, 0:E], x2T[:, :], w[:, W_R:W_R + E], start=True,
                                         stop=True).then_inc(lg_p, 1)
                    if has(0):
                        c = slice(GH * HD * g, GH * HD * (g + 1))
                        r = nc.tensor.matmul(bank[g][:, 0:GK], qT[c, u, :],
                                             kvbd[c, u, 0, :, :].rearrange("p a k -> p (a k)"), start=True, stop=True)
                        if g % 2:
                            r.then_inc(s_p, 1)
                if has(-2):
                    need(pe, on_d, i - 1)
                    need(pe, lg_d, i - 2)
                    nc.tensor.transpose(ps_b[:, 0:T], o_sb[:, :], ident).then_inc(oT_p, 1)

                def turn(f):
                    m = i - 1
                    need(pe, exp_d, m + 1)
                    need(pe, pt_d, FILLS * m + f)
                    for n in range(4):
                        g, c = divmod(4 * f + n, CH)
                        at = g * GK + 128 * c
                        r = nc.tensor.transpose(ps_p[:, n * T:(n + 1) * T], prob[:, o, at:at + 128], ident)
                    r.then_inc(pt_p, 1)

                def context(f):
                    m = i - 1
                    need(pe, pt_d, FILLS * m + f + 1)
                    if f == 0:
                        need(pe, vt_d, 2 * (m + 1))
                        need(pe, on_d, m)
                    for n in range(4):
                        g, c = divmod(4 * f + n, CH)
                        near = min(max(g - 1, 0), NG - 3)
                        at = g * GS - (g - near) * GC
                        r = nc.tensor.matmul(ps_o[:, at:at + 3 * GC], pT[:, f, n, :],
                                             vt[:, o, c, near:near + 3, :].rearrange("p g c -> p (g c)"),
                                             start=c == 0, stop=c == CH - 1)
                    r.then_inc(pv_p, 1)

                if has(-1):
                    turn(0)
                if has(1):
                    m = i + 1
                    need(pe, ctx_in[o], upto(m, o, 16) + 16)
                    need(pe, vt_d, 2 * m)
                    for n, wkv in enumerate((wk_sb, wv_sb)):
                        r = nc.tensor.matmul(ps_f[:, n * NKV:(n + 1) * NKV], wkv[:, :], ctx_sb[:, o, :],
                                             start=True, stop=True)
                    r.then_inc(kv_p, 1)
                if has(-2):
                    need(pe, oT_d, i - 1)
                    nc.tensor.matmul(ps_b[:, 0:D], oT[:, :], w[:, W_O:W_O + D], start=True, stop=True).then_inc(y_p, 1)
                if has(-1):
                    turn(1)
                    context(0)
                if has(1):
                    need(pe, kv_d, i + 2)
                    need(pe, xn_d, i + 2)
                    nc.tensor.transpose(ps_f[:, 0:T], xn[:, o, :], ident).then_inc(xnT_p, 1)
                if has(-1):
                    turn(2)
                if has(-3):
                    m = i - 3
                    need(pe, oh_d, m + 1)
                    need(pe, x1_d, m + 2 if has(-2) else 0)
                    for n, lhs in enumerate((tri, ones)):
                        for k in range(TOPK):
                            r = nc.tensor.matmul(ps_b[:, n * E:(n + 1) * E], lhs[:, :], onehot[:, k, :],
                                                 start=k == 0, stop=k == TOPK - 1)
                    r.then_inc(pre_p, 1)
                if has(-1):
                    context(1)
                if has(1):
                    need(pe, xnT_d, i + 2)
                    nc.tensor.matmul(ps_f[:, 0:T], w[:, W_Q:W_Q + D], xnT[:, o, :], start=True,
                                     stop=True).then_inc(q_p, 1)
                if has(-1):
                    context(2)
                if has(1):
                    need(pe, q_d, i + 2)
                    for c in range(CH):
                        n = min(128, GK - 128 * c)
                        r = nc.tensor.transpose(
                            ps_f[0:n, c * D:(c + 1) * D],
                            kvbd[:, o, 1, :, :].rearrange("p a k -> p (a k)")[:, 128 * c:128 * c + n], ident)
                    r.then_inc(vt_p, 1)
                if has(-2):
                    need(pe, x2_d, i - 1)
                    need(pe, base_d, i - 2)
                    nc.tensor.transpose(ps_b[:, 0:T], payload[:, u, 0, 0:D], ident).then_inc(x2T_p, 1)

            pipeline(pe, step)

            pe.wait_ge(s_moe, 32)
            pe.wait_ge(t_load, 32)

            def turn_x(t, u, loaded):
                need(pe, xin_in[u], loaded)
                nc.tensor.transpose(bank[u % 2][:, 0:128], xin[:, u, 0:D], ident).then_inc(xT_p, 1)

            def gate_up(t, u, e):
                need(pe, xT_d, t + 1)
                nc.tensor.matmul(bank[2 + u % 2][:, 0:2 * H], xT[:, u % 2, :], w_gu[:, bass.ds(e * (2 * H), 2 * H)],
                                 start=True, stop=True).then_inc(gu_p, 1)

            def turn_h(t, u):
                need(pe, h_d, t + 1)
                nc.tensor.transpose(bank[4 + u % 2][:, 0:128], h[:, u % 2, :], ident).then_inc(hT_p, 1)

            def down(t, u, e):
                need(pe, hT_d, t + 1)
                need(pe, y_d, t - 1)
                nc.tensor.matmul(bank[6 + u % 2][:, 0:D], hT[:, u % 2, :], w_dn[:, bass.ds(e * D, D)], start=True,
                                 stop=True).then_inc(dn_p, 1)

            def tiles(j, first=False, last=False):
                es = four(pe, exps_sb, j, 8, E - 1)
                loaded = 16 * j + 16 if isinstance(j, int) else pe.snap(16 * j + 16)
                for u in range(4):
                    t = 4 * j + u
                    gate_up(t, u, es[u])
                    if not (first and u == 0):
                        turn_h(t - 1, (u - 1) % 4)
                    if not (last and u == 3):
                        turn_x(t + 1, (u + 1) % 4, loaded if u < 3 else loaded + 16)
                    if not (first and u < 2):
                        down(t - 2, (u - 2) % 4, es[4 + u])
                return es

            turn_x(0, 0, 16)
            tiles(0, first=True)
            with pe.Fori(1, TG - 1) as j:
                tiles(j)
            es = tiles(TG - 1, last=True)
            turn_h(TILES - 1, 3)
            down(TILES - 2, 2, es[2])
            down(TILES - 1, 3, es[3])

            pe.wait_ge(sg_d, TILES)
            pe.wait_ge(h_d, TILES)
            pe.wait_ge(xT_d, TILES)
            pe.wait_ge(hT_d, TILES)
            pe.wait_ge(y_d, TILES)
            pe.wait_ge(x2Ta_d, B)

            def shared_up(c, n, u):
                need(pe, ssg_d, n - 1)
                need(pe, hs_d, n - 1)
                for which, (at, bk) in enumerate(((W_SG, u % 2), (W_SU, 2 + u % 2))):
                    nc.tensor.matmul(bank[bk][:, :], w[:, at + 128 * u:at + 128 * (u + 1)],
                                     x2T_all[:, bass.ds(c * 512, 512)], start=True, stop=True).then_inc(sg_p, 1)

            def shared_down(n, u):
                need(pe, hs_d, n + 1)
                for q in range(4):
                    if u == 0:
                        need(pe, take_d, n - 4 + q + 1)
                    nc.tensor.matmul(bank[4 + q][:, 0:D], hs[:, u % 2, q * 128:(q + 1) * 128],
                                     w[:, W_SD + 128 * u:W_SD + 128 * (u + 1)], start=u == 0,
                                     stop=u == NS - 1).then_inc(sy_p, 1)

            shared_up(0, 0, 0)
            for u in range(1, 4):
                shared_up(0, u, u)
                shared_down(u - 1, u - 1)
            with pe.Fori(1, B // 4) as c:
                for u in range(4):
                    shared_up(c, 4 * c + u, u)
                    shared_down(4 * c + u - 1, (u - 1) % 4)
            shared_down(B - 1, 3)


def kernel(**inp):
    import numpy as np
    import concourse.bacc as bacc
    from concourse.bass_utils import run_bass_kernel_spmd as run

    def arr(name):
        return np.asarray(inp[name])

    def rep(v):
        return np.broadcast_to(v, (128, v.size))

    p = np.arange(128)
    f = np.float32
    consts = np.zeros((128, C_END), f)
    consts[:, C_ID:C_ID + 128] = np.eye(128, dtype=f)
    consts[:, C_TRI:C_TRI + 128] = (p[:, None] < p[None, :])
    consts[:, C_ONE:C_ONE + 128] = 1
    consts[:, C_IOTA:C_IOTA + E] = np.arange(E)
    consts[:, C_EOFF:C_EOFF + E] = np.arange(E) * STRIDE
    consts[:, C_T:C_T + 8] = 4 * p[:, None] + np.array([0, 1, 2, 3, -2, -1, 0, 1])
    consts[:, C_DEST:C_DEST + TOPK] = p[:, None] * TOPK + np.arange(TOPK)
    consts[:, C_STEP:C_STEP + TOPK] = T * TOPK
    consts[:, C_PADD] = NOWHERE
    consts[:, C_P] = p
    consts[:, C_MASK:C_MASK + GH] = (p[:, None] // HD % GH == np.arange(GH))
    row = p[:, None] + 128 * np.arange(CH)
    consts[:, C_IND:C_IND + CH * GH] = (row[:, :, None] // NKV == np.arange(GH)).reshape(128, -1)
    sd = arr("L0_ffn_sdown_w").T.reshape(NS, 128, D).transpose(1, 0, 2).reshape(128, HS)
    wts = np.concatenate([arr("L0_xattn_Wq"), arr("L0_xattn_Wo"), arr("L0_ffn_router_w").T,
                          arr("L0_ffn_sgate_w").T, arr("L0_ffn_sup_w").T, sd], axis=1)
    vecs = np.concatenate([rep(arr("L0_ffn_router_bias")), rep(arr("L0_xattn_bo")),
                           arr("L0_xattn_bq")[:, None], rep(arr("g_xattn")), rep(arr("g_ffn"))], axis=1)
    ctxT = np.ones((CKV + 1, B * NKV), f)
    ctxT[:CKV] = arr("ctx_768").transpose(2, 0, 1).reshape(CKV, B * NKV)
    wk, wv = (np.concatenate([arr("L0_xattn_W" + c), arr("L0_xattn_b" + c)[None, :]]) for c in "kv")
    gu = np.concatenate([arr("L0_ffn_gate_w"), arr("L0_ffn_up_w")], axis=1).transpose(2, 0, 1).reshape(D, E * 2 * H)
    dn = arr("L0_ffn_down_w").transpose(2, 0, 1).reshape(H, E * D)
    ins = {
        "x": arr("x"),
        "ctxT": ctxT, "wk": wk, "wv": wv,
        "wts": wts, "vecs": vecs, "consts": consts, "gu": gu, "dn": dn,
    }
    ins = {k: np.ascontiguousarray(v) for k, v in ins.items()}
    nc = bacc.Bacc("TRN2", target_bir_lowering=False, num_devices=1)
    aps = [nc.dram_tensor(f"in_{k}", v.shape, mybir.dt.from_np(v.dtype), kind="ExternalInput").ap()
           for k, v in ins.items()]
    out = nc.dram_tensor("out", (B, T, D), F32, kind="ExternalOutput").ap()
    build(nc, *aps, out)
    r = run(nc, [{f"in_{k}": v for k, v in ins.items()}], core_ids=[0])
    return r.results[0]["out"]
```

```python
from contextlib import ExitStack

import concourse.bass as bass
from concourse import mybir

F32 = mybir.dt.float32
BF16 = mybir.dt.bfloat16
U32 = mybir.dt.uint32
I32 = mybir.dt.int32
ALU = mybir.AluOpType
ACT = mybir.ActivationFunctionType
AX_X = mybir.AxisListType.X

B, T, D = 64, 128, 128
NKV, CKV = 77, 96
NH = 16
HD = D // NH
CLAMP = 10000.0
EPS = 1e-5
E, H = 32, 128
TOPK = 4
HS = 512
NS = HS // 128
TOKENS = B * T
CHUNKS = B // 4
EARLY = 2
ROW = D + 1
STRIDE = TOKENS + 128
DUMMY = E * STRIDE
XROWS = DUMMY + 128
TILES = 288
U3 = 8
X_PARTS = (2, 14, 16, 32)
TG = TILES // U3
TW = 2 * U3 + 2
PADS_SP = 20
NOWHERE = 1 << 20

C_ID, C_TRI, C_ONE, C_IOTA, C_EOFF, C_T, C_DEST, C_STEP, C_PADD, C_P, C_MASK, C_IND, C_TIND, C_END = (
    0, 128, 256, 384, 416, 448, 458, 462, 466, 467, 468, 472, 480, 488)
W_Q, W_O, W_R, W_SG, W_SU, W_SD, W_END = 0, 128, 256, 288, 800, 1312, 1824
V_RB, V_BO, V_BQ, V_GX, V_GF, V_END = 0, 32, 160, 161, 162, 163
GH = 4
NG = NH // GH
GK = GH * NKV
CH = GK // 128
TAIL = GK - 128 * CH
FILLS = NG * CH // 4 + 1
GC = GH * HD + GH
GS = 4 * GC


def build(nc, x, ctxT, wkv, wts, vecs, consts, gu, dn, out):
    x_rows = nc.dram_tensor("x_rows", (XROWS, ROW), F32).ap()
    y_rows = nc.dram_tensor("y_rows", (TOKENS * TOPK, D), F32).ap()
    tab_dram = nc.dram_tensor("tab_dram", (TG, TW), I32).ap()

    with ExitStack() as stack:
        def sb(name, shape, dt=F32):
            return stack.enter_context(nc.sbuf_tensor(name, shape, dt))

        def sem(name):
            return stack.enter_context(nc.semaphore(name))

        def sems(name, n=2):
            return [sem(f"{name}{i}") for i in range(n)]

        cst = sb("cst", [128, C_END])
        w = sb("w", [128, W_END])
        vec = sb("vec", [128, V_END])
        wkv_sb = sb("wkv_sb", [CKV + 1, 2 * D])
        w_gu = sb("w_gu", [128, E * 2 * H])
        w_dn = sb("w_dn", [128, E * D])
        x_all = sb("x_all", [128, B * D])
        x2T_all = sb("x2T_all", [128, TOKENS])
        x2T = sb("x2T", [128, T])
        gates = sb("gates", [128, B * TOPK])
        tg = sb("tg", [128, 2])
        eps = sb("eps", [128, 1])
        bq_s = sb("bq_s", [128, 1])
        bias2 = sb("bias2", [128, D])
        tri = sb("tri", [128, 128], BF16)
        ones = sb("ones", [128, 128], BF16)
        base = sb("base", [128, 2, E])
        ident = cst[:, C_ID:C_ID + 128]
        iota = cst[:, C_IOTA:C_IOTA + E]

        ctx_sb = sb("ctx_sb", [CKV + 1, 2, NKV])
        st1 = sb("st1", [128, 2, 6])
        mv1 = sb("mv1", [128, 2, 2])
        lv1 = sb("lv1", [128, 2])
        rs1 = sb("rs1", [128, 2])
        xc = sb("xc", [128, D])
        xn = sb("xn", [128, 2, D])
        xnT = sb("xnT", [128, 2, T])
        kvbd = sb("kvbd", [128, 2, 2, GH, NKV])
        qT = sb("qT", [128, 2, NG, T])
        vt = sb("vt", [128, 2, CH, NG, GC])
        vtail = sb("vtail", [128, 2, NG // 2, 2, GC])
        mx = sb("mx", [128, NH])
        mxc = sb("mxc", [128, NH])
        prob = sb("prob", [128, 2, NG, GK])
        ptail = sb("ptail", [128, 2, NG, 64])
        pT = sb("pT", [128, FILLS, 4, T])
        rden = sb("rden", [128, NH])
        o_sb = sb("o_sb", [128, D])
        oT = sb("oT", [128, T])
        st2 = sb("st2", [128, 6])
        mv2 = sb("mv2", [128, 2])
        lv2 = sb("lv2", [128, 1])
        rs2 = sb("rs2", [128, 1])
        payload = sb("payload", [128, 2, TOPK, ROW])
        lg = sb("lg", [128, E])
        top = sb("top", [128, 8])
        ntop = sb("ntop", [128, 1])
        idx = sb("idx", [128, 8], U32)
        idxf = sb("idxf", [128, TOPK])
        onehot = sb("onehot", [128, TOPK, E], BF16)
        e4 = sb("e4", [128, TOPK])
        se4 = sb("se4", [128, 1])
        rse4 = sb("rse4", [128, 1])
        pos = sb("pos", [128, E])
        prod = sb("prod", [128, TOPK, E])
        slotf = sb("slotf", [128, TOPK])
        slot = sb("slot", [128, 2, TOPK], U32)
        dest = sb("dest", [128, 2, TOPK])

        cnt = sb("cnt", [128, E])
        cnti = sb("cnti", [128, E], I32)
        ntilei = sb("ntilei", [128, E], I32)
        ntile = sb("ntile", [128, E])
        ends = sb("ends", [128, E])
        starts = sb("starts", [128, E])
        adj = sb("adj", [128, E])
        past = sb("past", [128, U3 + 2, E])
        et = sb("et", [128, U3 + 2])
        valid = sb("valid", [128, U3])
        oht = sb("oht", [128, U3, E])
        srow = sb("srow", [128, U3])
        trow = sb("trow", [128, U3])
        row2 = sb("row2", [128, U3])
        tab = sb("tab", [128, TW], I32)
        basei = sb("basei", [1, E], I32)
        padidx = sb("padidx", [128, E], U32)
        tab_sb = sb("tab_sb", [1, TG * TW], I32)
        pad = sb("pad", [128, ROW])

        xin = sb("xin", [128, U3, ROW])
        xT = sb("xT", [128, 2, 128])
        sg = sb("sg", [128, 2, H])
        h = sb("h", [128, 2, H])
        hT = sb("hT", [128, 2, 128])
        y_sb = sb("y_sb", [128, U3, D])
        didx = sb("didx", [128, U3], U32)

        ssg = sb("ssg", [128, 2, 512])
        hs = sb("hs", [128, 2, 512])
        yld = w_gu[:, 0:8 * TOPK * D].rearrange("p (s q k d) -> p s q k d", s=2, q=4, k=TOPK)
        acc = w_gu[:, 8 * TOPK * D:8 * (TOPK + 2) * D].rearrange("p (s k q d) -> p s k q d", s=2, k=2, q=4)

        ps = stack.enter_context(nc.psum_tensor("ps", [128, 8, 512], F32))
        bank = [ps[:, i, :] for i in range(8)]
        ps_p, ps_o, ps_f, ps_b = bank[4:8]
        ov = ps[:, 5:7, :].rearrange("p b n -> p (b n)")[:, 0:NG * GS].rearrange("p (g c) -> p g c", c=GS)

        s_cst, s_w, s_vec, s_wkv, s_moe = sem("s_cst"), sem("s_w"), sem("s_vec"), sem("s_wkv"), sem("s_moe")
        s_x = sems("s_x", 4)
        s_zero, s_tg, s_eps, s_bq, s_b2g = (sem(n) for n in ("s_zero", "s_tg", "s_eps", "s_bq", "s_b2g"))
        s_tri, s_base0, s_dest0, s_pad = sem("s_tri"), sem("s_base0"), sem("s_dest0"), sem("s_pad")
        ctx_in, sent = sems("ctx_in"), sems("sent")
        names = ("st1_d mv1_d lv1_d rs1_d xc_d xn_d xnT_p xnT_d kv_p kv_d q_p q_d vt_p vt_d s_p mx_d mxc_d diff_d relu_d "
                 "exp_d pt_p pt_d pv_p rden_d on_d oT_p oT_d y_p xb_d x1_d st2_d mv2_d lv2_d rs2_d x2_d x2T_p x2T_d x2Ta_d "
                 "lg_p lg_d top_d ntop_d idx_d idxf_d oh_d pre_p pos_d base_d prod_d slotf_d slot_d e4_d "
                 "rse_d gate_d pidx_d dest_d")
        S = {n: sem(n) for n in names.split()}
        (st1_d, mv1_d, lv1_d, rs1_d, xc_d, xn_d, xnT_p, xnT_d, kv_p, kv_d, q_p, q_d, vt_p, vt_d, s_p, mx_d, mxc_d, diff_d,
         relu_d, exp_d, pt_p, pt_d, pv_p, rden_d, on_d, oT_p, oT_d, y_p, xb_d, x1_d, st2_d, mv2_d, lv2_d, rs2_d,
         x2_d, x2T_p, x2T_d, x2Ta_d, lg_p, lg_d, top_d, ntop_d, idx_d, idxf_d, oh_d, pre_p, pos_d, base_d, prod_d,
         slotf_d, slot_d, e4_d, rse_d, gate_d, pidx_d, dest_d) = S.values()
        t_step, t_tab, t_store, t_load, t_padded, t_padded2, t_basei, t_padidx = (sem(n) for n in (
            "t_step", "t_tab", "t_store", "t_load", "t_padded", "t_padded2", "t_basei", "t_padidx"))
        xin_in, y_sent = sems("xin_in", U3), sems("y_sent", U3)
        xT_p, xT_d, gu_p, sg_d, h_d, hT_p, hT_d, dn_p, y_d, didx_d = (sems(n, 4) for n in (
            "xT_p", "xT_d", "gu_p", "sg_d", "h_d", "hT_p", "hT_d", "dn_p", "y_d", "didx_d"))
        yld_in, out_sent = sems("yld_in"), sems("out_sent")
        sg_p, ssg_d, hs_d, sy_p, take_d, acc_d = (sem(n) for n in ("sg_p", "ssg_d", "hs_d", "sy_p", "take_d", "acc_d"))

        def need(eng, s, count):
            if not isinstance(count, int) or count > 0:
                eng.wait_ge(s, count)

        passed = sem("passed")

        def need_first(eng, s, count):
            need(eng, s, count)
            if not isinstance(count, int):
                eng.sem_inc(passed, 1)

        def pipeline(eng, step):
            for i in range(-2, 4):
                step(i, i % 2, lambda k, i=i: 0 <= i + k < B)
            with eng.Fori(1, B // 4 - 1) as j:
                for u in range(4):
                    step(4 * j + u, u % 2, lambda k: True)
            for i in range(B - 4, B + 3):
                step(i, i % 2, lambda k, i=i: 0 <= i + k < B)

        def upto(m, u, each, slots=2):
            return each * ((m - u) // slots) if isinstance(m, int) else each // slots * (m - u)

        def counts(eng, j, last=0, dma=False):
            per_body, each = (1, 16) if dma else (U3 // 4, 1)
            return [each * (per_body * j + k) if isinstance(j, int) else eng.snap(each * (per_body * j + k))
                    for k in range(last + 1)]

        def tile_done(eng, places, n, u):
            need(eng, places[u % len(places)], n[u // len(places) + 1])

        def numbers(eng, numbers_sb, at, n, top):
            return nc.values_load_multi_w_load_instructions(
                numbers_sb[0:1, bass.ds(at, n)], engines=[eng.engine], min_val=0, max_val=top,
                skip_runtime_bounds_check_because="the table is computed within its bounds")[1]

        block = stack.enter_context(nc.Block())

        @block.sync
        def _(sp):
            xv = x.rearrange("b t d -> t b d")

            def load_x(q):
                first, n = sum(X_PARTS[:q]), X_PARTS[q]
                sp.dma_start(x_all[:, first * D:(first + n) * D].rearrange("p (b d) -> p b d", d=D),
                             xv[:, first:first + n, :]).then_inc(s_x[q], 16)

            def load_ctx(m, u):
                sp.dma_start(ctx_sb[:, u, :], ctxT[:, bass.ds(m * NKV, NKV)]).then_inc(ctx_in[u], 16)

            load_x(0)
            sp.dma_start(vec[:, :], vecs).then_inc(s_vec, 16)
            sp.dma_start(cst[:, :], consts).then_inc(s_cst, 16)
            sp.dma_start(wkv_sb[:, :], wkv).then_inc(s_wkv, 16)
            load_ctx(0, 0)
            sp.dma_start(w[:, 0:W_SG], wts[:, 0:W_SG]).then_inc(s_w, 16)
            load_ctx(1, 1)
            load_x(1)
            sp.wait_ge(s_pad, 3)
            sp.dma_start(x_rows[DUMMY:DUMMY + 128, :], pad[:, :]).then_inc(t_padded, 16)

            half = E * H
            later = {0: lambda: load_x(2),
                     1: lambda: load_x(3),
                     2: lambda: sp.dma_start(w_gu[:, 0:half], gu[:, 0:half]).then_inc(s_moe, 16),
                     3: lambda: sp.dma_start(w_gu[:, half:], gu[:, half:]).then_inc(s_moe, 16),
                     B - 4: lambda: sp.dma_start(w[:, W_SG:], wts[:, W_SG:]).then_inc(s_moe, 16),
                     B - 3: lambda: sp.dma_start(w_dn[:, :], dn).then_inc(s_moe, 16)}

            def step(i, u, has):
                if has(2) and not (isinstance(i, int) and i < 0):
                    need(sp, kv_p, i + 1)
                    load_ctx(i + 2, u)
                if isinstance(i, int) and i in later:
                    later[i]()

            pipeline(sp, step)

            sp.wait_ge(t_basei, 1)

            def paddings(e):
                for first in numbers(sp, basei, 4 * e, 4, XROWS - 128):
                    sp.dma_start(x_rows[bass.ds(first, 128), :], pad[:, :]).then_inc(t_padded, 16)

            with sp.Fori(0, 2) as e:
                paddings(e)
            sp.wait_ge(t_tab, 2)
            sp.dma_start(tab_dram, tab[0:TG, :]).then_inc(t_store, 16)
            with sp.Fori(2, PADS_SP // 4) as e:
                paddings(e)
            sp.wait_ge(t_store, 16)
            sp.dma_start(tab_sb[:, :], tab_dram.rearrange("(o n) k -> o (n k)", o=1)).then_inc(t_load, 16)
            sp.wait_ge(t_load, 16)
            sp.wait_ge(t_padded, 16 * (PADS_SP + 1))
            sp.wait_ge(t_padded2, 16 * (E - PADS_SP))
            for u in range(2):
                sp.wait_ge(sent[u], 64 * (B // 2))

            def load_tiles(j):
                firsts = numbers(sp, tab_sb, j * TW, U3, XROWS - 128)
                n = counts(sp, j - 1, U3 // 4) if not isinstance(j, int) or j else [0] * U3
                for u in range(U3):
                    tile_done(sp, didx_d, n, u)
                    sp.dma_start(xin[:, u, :], x_rows[bass.ds(firsts[u], 128), :]).then_inc(xin_in[u], 16)

            load_tiles(0)
            with sp.Fori(1, TG) as j:
                load_tiles(j)

            for u in range(U3):
                sp.wait_ge(y_sent[u], 16 * TG)
            yv = y_rows.rearrange("(t p k) d -> p t (k d)", p=T, k=TOPK)
            outv = out.rearrange("b t d -> t b d")

            def load_y(c, v):
                need(sp, acc_d, 4 * TOPK * (c - 1))
                sp.dma_start(yld[:, v, :, :, :].rearrange("p q k d -> p q (k d)"),
                             yv[:, bass.ds(4 * c, 4), :]).then_inc(yld_in[v], 16)

            def store(c, v):
                need(sp, acc_d, 4 * TOPK * (c + 1))
                sp.dma_start(outv[:, bass.ds(4 * c, 4), :], acc[:, v, 0, :, :]).then_inc(out_sent[v], 16)

            for v in range(2):
                load_y(v, v)
            with sp.Fori(0, CHUNKS // 2 - 1) as j:
                for v in range(2):
                    store(2 * j + v, v)
                    load_y(2 * j + v + 2, v)
            for v in range(2):
                store(CHUNKS - 2 + v, v)
            for v in range(2):
                sp.wait_ge(out_sent[v], 16 * (CHUNKS // 2))

        @block.gpsimd
        def _(pool):
            pool.wait_ge(s_cst, 16)
            nc.gpsimd.tensor_copy(dest[:, 1, :], cst[:, C_DEST:C_DEST + TOPK]).then_inc(s_dest0, 1)
            nc.gpsimd.memset(pad[:, 0:D], 0.0).then_inc(s_pad, 1)
            pool.wait_ge(s_pad, 1)
            nc.gpsimd.tensor_copy(pad[:, D:ROW].bitcast(U32), cst[:, C_PADD:C_PADD + 1]).then_inc(s_pad, 2)

            pool.wait_ge(s_b2g, 1)
            pool.wait_ge(s_dest0, 1)

            def step(i, u, has):
                o = 1 - u
                if isinstance(i, int) and i in (-2, 0, 3):
                    for q in {-2: (0,), 0: (1,), 3: (2, 3)}[i]:
                        pool.wait_ge(s_x[q], 16)
                if has(0):
                    need_first(pool, xn_d, i + 1)
                    xi = x_all[:, bass.ds(i * D, D)]
                    nc.gpsimd.tensor_tensor(xi, xi, bias2[:, :], ALU.add).then_inc(xb_d, 1)
                if has(2):
                    m = i + 2
                    need(pool, rs1_d, m + 1)
                    need(pool, xnT_p, m - 1)
                    need_first(pool, xn_d, m)
                    nc.gpsimd.tensor_tensor(xc[:, :], x_all[:, bass.ds(m * D, D)],
                                            mv1[:, u, 0:1].broadcast_to([128, D]), ALU.subtract).then_inc(xc_d, 1)
                    need(pool, xc_d, m + 1)
                    nc.gpsimd.tensor_tensor(xn[:, u, :], xc[:, :], rs1[:, u:u + 1].broadcast_to([128, D]),
                                            ALU.mult).then_inc(xn_d, 1)
                if has(-3):
                    m, v = i - 3, o
                    need(pool, pos_d, m + 1)
                    nc.gpsimd.tensor_tensor(prod[:, :, :], onehot[:, :, :],
                                            pos[:, :].unsqueeze(1).broadcast_to([128, TOPK, E]),
                                            ALU.mult).then_inc(prod_d, 1)
                    need(pool, sent[v], upto(m, v, 64))
                    need_first(pool, dest_d, m)
                    nc.gpsimd.tensor_copy(payload[:, v, :, D:ROW].rearrange("p k o -> p (k o)").bitcast(U32),
                                          dest[:, 1 - v, :]).then_inc(pidx_d, 1)
                    need(pool, pidx_d, m + 1)
                    nc.gpsimd.tensor_tensor(dest[:, v, :], dest[:, 1 - v, :], cst[:, C_STEP:C_STEP + TOPK],
                                            ALU.add).then_inc(dest_d, 1)
                    need_first(pool, slot_d, m + 1)
                    for k in range(TOPK):
                        nc.gpsimd.indirect_dma_start(
                            x_rows, bass.IndirectOffsetOnAxis(ap=slot[:, v, k:k + 1], axis=0),
                            payload[:, v, k, :], None).then_inc(sent[v], 16)

            pipeline(pool, step)

            pool.wait_ge(t_padidx, 1)
            pool.wait_ge(s_pad, 3)
            for e in range(PADS_SP, E):
                nc.gpsimd.indirect_dma_start(x_rows, bass.IndirectOffsetOnAxis(ap=padidx[:, e:e + 1], axis=0),
                                             pad[:, :], None).then_inc(t_padded2, 16)

            def scatter(n, u):
                if u % 2 == 0:
                    need_first(pool, y_d[(u + 1) % 4], n[(u + 1) // 4 + 1])
                nc.gpsimd.indirect_dma_start(
                    y_rows, bass.IndirectOffsetOnAxis(ap=didx[:, u:u + 1], axis=0), y_sb[:, u, :], None,
                    bounds_check=TOKENS * TOPK - 1, oob_is_err=False).then_inc(y_sent[u], 16)

            with pool.Fori(0, TG) as j:
                n = counts(pool, j, U3 // 4)
                for u in range(U3):
                    scatter(n, u)

        @block.scalar
        def _(act):
            act.wait_ge(s_vec, 16)
            nc.scalar.activation(tg[:, :], vec[:, V_GX:V_GF + 1], ACT.Tanh).then_inc(s_tg, 1)
            nc.scalar.mul(bq_s[:, :], vec[:, V_BQ:V_BQ + 1], HD ** -0.5).then_inc(s_bq, 1)
            nc.scalar.preload_act_table_set("natural_log_exp_and_others")
            act.wait_ge(s_bq, 1)
            act.wait_ge(s_eps, 1)
            act.wait_ge(s_zero, 3)

            def step(i, u, has):
                o = 1 - u

                def relu(n):
                    p = prob[:, u, 2 * n:2 * n + 2, :]
                    need(act, diff_d, 2 * i + n + 1)
                    nc.scalar.activation(p, p, ACT.Relu, scale=-1.0).then_inc(relu_d, 1)

                def exp(n):
                    need(act, relu_d, 2 * i + n + 1)
                    p = prob[:, u, 2 * n:2 * n + 2, 0:128 * CH]
                    nc.scalar.activation(p, p, ACT.Exp, scale=-1.0).then_inc(exp_d, 1)

                def exp_tails():
                    need(act, relu_d, 2 * i)
                    nc.scalar.activation(ptail[:, o, :, 0:TAIL], prob[:, o, :, 128 * CH:GK], ACT.Exp,
                                         scale=-1.0).then_inc(exp_d, 1)

                def fill(f):
                    n = 4 if f < FILLS - 1 else NG // 2
                    need(act, pt_p, FILLS * (i - 1) + f + 1)
                    need(act, pv_p, FILLS * (i - 2) + f + 1)
                    nc.scalar.copy(pT[:, f, 0:n, :].rearrange("p a b -> p (a b)"), ps_p[:, 0:n * T]).then_inc(pt_d, 1)

                if has(-1):
                    exp_tails()
                if has(2):
                    m = i + 2
                    need(act, mv1_d, m + 1)
                    need(act, xn_d, m - 1)
                    nc.scalar.activation(lv1[:, u:u + 1], mv1[:, u, 1:2], ACT.Ln, bias=eps[:, :]).then_inc(lv1_d, 1)
                    need(act, lv1_d, m + 1)
                    nc.scalar.activation(rs1[:, u:u + 1], lv1[:, u:u + 1], ACT.Exp, scale=-0.5).then_inc(rs1_d, 1)
                if has(-1):
                    fill(0)
                if has(1):
                    need(act, xnT_p, i + 2)
                    need(act, q_p, i)
                    nc.scalar.copy(xnT[:, o, :], ps_f[:, 0:T]).then_inc(xnT_d, 1)
                if has(-2):
                    need(act, oT_p, i - 1)
                    need(act, y_p, i - 2)
                    nc.scalar.copy(oT[:, :], ps_b[:, 0:T]).then_inc(oT_d, 1)

                if has(-3):
                    need(act, ntop_d, i - 2)
                    need(act, gate_d, i - 3)
                    nc.scalar.activation(e4[:, :], top[:, 0:TOPK], ACT.Exp, bias=ntop[:, :],
                                         accum_out=se4[:, :]).then_inc(e4_d, 1)
                if has(-1):
                    fill(1)
                if has(1):
                    need(act, q_p, i + 2)
                    need(act, s_p, 2 * i)
                    for g in range(NG):
                        c = slice(GH * HD * g, GH * HD * (g + 1))
                        r = nc.scalar.activation(qT[c, o, g, :], ps_f[c, 0:T], ACT.Identity, bias=bq_s[c, :],
                                                 scale=HD ** -0.5)
                    r.then_inc(q_d, 1)
                if has(0):
                    relu(0)
                if has(-2):
                    need(act, mv2_d, i - 1)
                    need(act, x2_d, i - 2)
                    nc.scalar.activation(lv2[:, :], mv2[:, 1:2], ACT.Ln, bias=eps[:, :]).then_inc(lv2_d, 1)
                if has(-1):
                    fill(2)
                if has(-2):
                    need(act, lv2_d, i - 1)
                    nc.scalar.activation(rs2[:, :], lv2[:, :], ACT.Exp, scale=-0.5).then_inc(rs2_d, 1)
                if has(0):
                    relu(1)
                if has(1):
                    need(act, vt_p, i + 2)
                    need(act, pv_p, FILLS * i)
                    nc.scalar.copy(vt[:, o, :, :, 0:GH * HD],
                                   ps_f[:, 0:CH * D].rearrange("p (c g d) -> p c g d", c=CH, g=NG))
                    for m in range(2):
                        rows = slice(64 * m, 64 * m + TAIL)
                        r = nc.scalar.copy(vtail[rows, o, :, m, 0:GH * HD],
                                           ps_f[rows, CH * D:(CH + 1) * D].rearrange(
                                               "p (g m d) -> p g m d", m=2, d=GH * HD)[:, :, m, :])
                    r.then_inc(vt_d, 1)
                if has(0):
                    exp(0)
                if has(-2):
                    need(act, x2T_p, i - 1)
                    need(act, lg_p, i - 2)
                    nc.scalar.copy(x2T[:, :], ps_b[:, 0:T]).then_inc(x2T_d, 1)
                    nc.scalar.copy(x2T_all[:, bass.ds((i - 2) * T, T)], ps_b[:, 0:T]).then_inc(x2Ta_d, 1)
                if has(0):
                    exp(1)

            pipeline(act, step)

            nc.scalar.preload_act_table(ACT.Silu)

            def ssilu(n, u):
                need(act, sg_p, 2 * n + 1)
                need(act, hs_d, n - 1)
                nc.scalar.activation(ssg[:, u % 2, :], bank[u % 2][:, :], ACT.Silu).then_inc(ssg_d, 1)

            for n in range(4 * EARLY):
                ssilu(n, n % 4)

            def evac(n, u):
                tile_done(act, xT_p, n, u)
                nc.scalar.copy(xT[:, u % 2, :], bank[u % 2][:, 0:128]).then_inc(xT_d[u % 4], 1)

            def silu(n, u):
                tile_done(act, gu_p, n, u)
                nc.scalar.activation(sg[:, u % 2, :], bank[2 + u % 2][:, 0:H], ACT.Silu).then_inc(sg_d[u % 4], 1)

            def h_turned(n, u):
                tile_done(act, hT_p, n, u)
                nc.scalar.copy(hT[:, u % 2, :], bank[4 + u % 2][:, 0:128]).then_inc(hT_d[u % 4], 1)

            def body(j, first=False, last=False):
                n = counts(act, j, U3 // 4 + 1)
                for u in range(U3):
                    silu(n, u)
                    if not (first and u == 0):
                        h_turned(n, u - 1)
                    if not (last and u >= U3 - 2):
                        evac(n, u + 2)

            for u in range(2):
                evac(counts(act, 0, 1), u)
            body(0, first=True)
            with act.Fori(1, TG - 1) as j:
                body(j)
            body(TG - 1, last=True)
            h_turned(counts(act, TG - 1, U3 // 4), U3 - 1)

            with act.Fori(EARLY, CHUNKS) as j:
                for u in range(4):
                    ssilu(4 * j + u, u)

        @block.vector
        def _(dve):
            nc.vector.memset(ptail[:, :, :, :], 0.0).then_inc(s_zero, 1)
            nc.vector.memzero(vt[:, :, :, :, :])
            nc.vector.memzero(vtail[:, :, :, :, :]).then_inc(s_zero, 1)
            nc.vector.memzero(qT[:, :, :, :]).then_inc(s_zero, 1)
            nc.vector.memset(eps[:, :], EPS).then_inc(s_eps, 1)
            dve.wait_ge(s_cst, 16)
            nc.vector.tensor_copy(tri[:, :], cst[:, C_TRI:C_TRI + 128]).then_inc(s_tri, 1)
            nc.vector.tensor_copy(ones[:, :], cst[:, C_ONE:C_ONE + 128]).then_inc(s_tri, 1)
            nc.vector.tensor_copy(base[:, 0, :], cst[:, C_EOFF:C_EOFF + E]).then_inc(s_base0, 1)
            dve.wait_ge(s_zero, 3)
            for n in range(2):
                for g in range(NG):
                    nc.vector.tensor_copy(vt[:, n, :, g, GH * HD:GC],
                                          cst[:, C_IND:C_IND + CH * GH].rearrange("p (c a) -> p c a", c=CH))
                for g in range(NG // 2):
                    r = nc.vector.tensor_copy(vtail[:, n, g, :, GH * HD:GC],
                                              cst[:, C_TIND:C_TIND + 2 * GH].rearrange("p (m a) -> p m a", m=2))
            r.then_inc(s_zero, 1)
            dve.wait_ge(s_vec, 16)
            dve.wait_ge(s_tg, 1)
            nc.vector.tensor_scalar(bias2[:, :], vec[:, V_BO:V_BO + D], tg[:, 0:1], None, ALU.mult).then_inc(s_b2g, 1)
            dve.wait_ge(s_base0, 1)
            mask = cst[:, C_MASK:C_MASK + GH].unsqueeze(1).unsqueeze(3).broadcast_to([128, 2, GH, NKV])

            def step(i, u, has):
                o = 1 - u
                if isinstance(i, int) and i in (-2, 0, 3):
                    for q in {-2: (0,), 0: (1,), 3: (2, 3)}[i]:
                        dve.wait_ge(s_x[q], 16)
                if has(-2):
                    m = i - 2
                    need(dve, pv_p, FILLS * (m + 1))
                    nc.vector.reciprocal(rden[:, :].rearrange("p (g a) -> p g a", a=GH),
                                         ov[:, :, GH * HD:GC]).then_inc(rden_d, 1)
                if has(2):
                    m = i + 2
                    nc.vector.bn_stats(st1[:, u, :], x_all[:, bass.ds(m * D, D)]).then_inc(st1_d, 1)
                if has(-2):
                    need(dve, rden_d, i - 1)
                    need(dve, oT_p, i - 2)
                    nc.vector.tensor_tensor(
                        o_sb[:, :].rearrange("p (g a d) -> p g a d", a=GH, d=HD),
                        ov[:, :, 0:GH * HD].rearrange("p g (a d) -> p g a d", a=GH),
                        rden[:, :].rearrange("p (g a) -> p g a", a=GH).unsqueeze(3).broadcast_to([128, NG, GH, HD]),
                        ALU.mult).then_inc(on_d, 1)
                if has(2):
                    need(dve, xn_d, i + 1)
                    need_first(dve, st1_d, i + 3)
                    nc.vector.bn_aggr(mv1[:, u, :], st1[:, u, :]).then_inc(mv1_d, 1)

                def maxima(n):
                    need(dve, s_p, 2 * i + n + 1)
                    nc.vector.reduce_max(mx[:, 2 * GH * n:2 * GH * (n + 1)].rearrange("p (g a) -> p g a", a=GH),
                                         ps[:, 2 * n:2 * n + 2, 0:GK].rearrange("p g (a k) -> p g a k", k=NKV),
                                         AX_X).then_inc(mx_d, 1)

                if has(0):
                    maxima(0)
                if has(-3):
                    need(dve, lg_p, i - 2)
                    nc.vector.tensor_tensor(lg[:, :], ps_b[:, 0:E], vec[:, V_RB:V_RB + E], ALU.add).then_inc(lg_d, 1)
                if has(1):
                    m = i + 1
                    need(dve, kv_p, m + 1)
                    need(dve, vt_p, m - 1)
                    nc.vector.tensor_tensor(
                        kvbd[:, o, :, :, :],
                        ps_f[:, 0:2 * NKV].rearrange("p (n k) -> p n k", n=2).unsqueeze(2).broadcast_to(
                            [128, 2, GH, NKV]), mask, ALU.mult).then_inc(kv_d, 1)
                if has(-3):
                    m = i - 3
                    need(dve, lg_d, m + 1)
                    need_first(dve, e4_d, m)
                    nc.vector.max(top[:, :], lg[:, :]).then_inc(top_d, 1)
                    need(dve, top_d, m + 1)
                    nc.vector.tensor_scalar(ntop[:, :], top[:, 0:1], -1.0, None, ALU.mult).then_inc(ntop_d, 1)
                    nc.vector.max_index(idx[:, :], top[:, :], lg[:, :]).then_inc(idx_d, 1)
                if has(0):
                    maxima(1)
                if has(-3):
                    need(dve, idx_d, i - 2)
                    nc.vector.tensor_copy(idxf[:, :], idx[:, 0:TOPK]).then_inc(idxf_d, 1)
                if has(0):
                    need(dve, mx_d, 2 * i + 2)
                    nc.vector.tensor_scalar(mxc[:, :], mx[:, :], -CLAMP, CLAMP, ALU.max, ALU.min).then_inc(mxc_d, 1)
                if has(-3):
                    m = i - 3
                    need(dve, idxf_d, m + 1)
                    need(dve, pre_p, m)
                    nc.vector.tensor_tensor(onehot[:, :, :], iota.unsqueeze(1).broadcast_to([128, TOPK, E]),
                                            idxf[:, :].unsqueeze(2).broadcast_to([128, TOPK, E]),
                                            ALU.is_equal).then_inc(oh_d, 1)
                xi = x_all[:, bass.ds((i - 2) * D, D)] if has(-2) else None
                def difference(n):
                    nc.vector.scalar_tensor_tensor(
                        out=prob[:, u, 2 * n:2 * n + 2, :].rearrange("p g (a k) -> p g a k", a=GH),
                        in0=ps[:, 2 * n:2 * n + 2, 0:GK].rearrange("p g (a k) -> p g a k", k=NKV), scalar=-CLAMP,
                        in1=mxc[:, 2 * GH * n:2 * GH * (n + 1)].rearrange("p (g a) -> p g a", a=GH).unsqueeze(
                            3).broadcast_to([128, 2, GH, NKV]),
                        op0=ALU.max, op1=ALU.subtract).then_inc(diff_d, 1)

                if has(-2):
                    need(dve, y_p, i - 1)
                    need(dve, xb_d, i - 1)
                    nc.vector.scalar_tensor_tensor(out=xi, in0=ps_b[:, 0:D], scalar=tg[:, 0:1], in1=xi,
                                                   op0=ALU.mult, op1=ALU.add).then_inc(x1_d, 1)

                if has(0):
                    need(dve, mxc_d, i + 1)
                    need(dve, pt_p, FILLS * (i - 1))
                    difference(0)
                if has(-2):
                    need_first(dve, x1_d, i - 1)
                    nc.vector.bn_stats(st2[:, :], xi).then_inc(st2_d, 1)
                if has(-3):
                    m, v = i - 3, o
                    need(dve, pre_p, m + 1)
                    need(dve, base_d, m)
                    nc.vector.tensor_tensor(pos[:, :], ps_b[:, 0:E], base[:, v, :], ALU.add).then_inc(pos_d, 1)
                    nc.vector.tensor_tensor(base[:, 1 - v, :], ps_b[:, E:2 * E], base[:, v, :],
                                            ALU.add).then_inc(base_d, 1)
                if has(-2):
                    need_first(dve, st2_d, i - 1)
                    nc.vector.bn_aggr(mv2[:, :], st2[:, :]).then_inc(mv2_d, 1)
                if has(0):
                    difference(1)
                if has(-3):
                    need(dve, e4_d, i - 2)
                    nc.vector.reciprocal(rse4[:, :], se4[:, :]).then_inc(rse_d, 1)
                if has(-2):
                    m = i - 2
                    need(dve, rs2_d, m + 1)
                    need(dve, sent[u], upto(m, u, 64))
                    nc.vector.tensor_scalar(payload[:, u, :, 0:D], xi.unsqueeze(1).broadcast_to([128, TOPK, D]),
                                            mv2[:, 0:1], rs2[:, :], ALU.subtract, ALU.mult).then_inc(x2_d, 1)
                if has(-3):
                    m, v = i - 3, o
                    need(dve, prod_d, m + 1)
                    nc.vector.reduce_sum(slotf[:, :], prod[:, :, :], AX_X).then_inc(slotf_d, 1)
                    need(dve, rse_d, m + 1)
                    nc.vector.tensor_scalar(gates[:, bass.ds(m * TOPK, TOPK)], e4[:, :], rse4[:, :], tg[:, 1:2],
                                            ALU.mult, ALU.mult).then_inc(gate_d, 1)
                    need(dve, slotf_d, m + 1)
                    nc.vector.tensor_copy(slot[:, v, :], slotf[:, :]).then_inc(slot_d, 1)

            pipeline(dve, step)

            def shared_hidden(n, u):
                need(dve, ssg_d, n + 1)
                need(dve, sg_p, 2 * n + 2)
                need(dve, sy_p, 4 * (n - 1))
                nc.vector.tensor_tensor(hs[:, u % 2, :], ssg[:, u % 2, :], bank[2 + u % 2][:, :],
                                        ALU.mult).then_inc(hs_d, 1)

            def take(c):
                for q in range(4):
                    xq = x_all[:, bass.ds((4 * c + q) * D, D)]
                    need(dve, sy_p, 16 * c + 12 + q + 1)
                    nc.vector.scalar_tensor_tensor(out=xq, in0=bank[4 + q][:, 0:D], scalar=tg[:, 1:2], in1=xq,
                                                   op0=ALU.mult, op1=ALU.add).then_inc(take_d, 1)

            steps = [0]

            def link(ins):
                steps[0] += 1
                ins.then_inc(t_step, 1)
                dve.wait_ge(t_step, steps[0])

            last = base[:, B % 2, :]
            dve.wait_ge(base_d, B)
            nc.vector.tensor_copy(basei[:, :], base[0:1, B % 2, :]).then_inc(t_basei, 1)
            nc.vector.tensor_scalar(padidx[:, :], last, cst[:, C_P:C_P + 1], None, ALU.add).then_inc(t_padidx, 1)
            link(nc.vector.tensor_tensor(cnt[:, :], last, cst[:, C_EOFF:C_EOFF + E], ALU.subtract))
            link(nc.vector.tensor_scalar(cnti[:, :], cnt[:, :], 127.0, None, ALU.add))
            link(nc.vector.tensor_single_scalar(ntilei[:, :], cnti[:, :], 7, ALU.logical_shift_right))
            link(nc.vector.tensor_copy(ntile[:, :], ntilei[:, :]))
            link(nc.vector.tensor_tensor_scan(ends[:, :], cst[:, C_ONE:C_ONE + E], ntile[:, :], 0.0,
                                              ALU.mult, ALU.add))
            link(nc.vector.tensor_tensor(starts[:, :], ends[:, :], ntile[:, :], ALU.subtract))
            link(nc.vector.scalar_tensor_tensor(out=adj[:, :], in0=starts[:, :], scalar=-128.0,
                                                in1=cst[:, C_EOFF:C_EOFF + E], op0=ALU.mult, op1=ALU.add))
            tnum = cst[:, C_T:C_T + U3 + 2]
            wide = [128, U3 + 2, E]
            link(nc.vector.tensor_tensor(past[:, :, :], tnum.unsqueeze(2).broadcast_to(wide),
                                         ends[:, :].unsqueeze(1).broadcast_to(wide), ALU.is_ge))
            link(nc.vector.reduce_sum(et[:, :], past[:, :, :], AX_X))
            nc.vector.tensor_scalar(tab[:, U3:TW], et[:, :], float(E - 1), None, ALU.min).then_inc(t_tab, 1)
            shared_hidden(0, 0)
            half = [128, U3, E]
            link(nc.vector.tensor_scalar(valid[:, :], et[:, 2:], float(E), None, ALU.is_lt))
            link(nc.vector.tensor_tensor(oht[:, :, :], iota.unsqueeze(1).broadcast_to(half),
                                         et[:, 2:].unsqueeze(2).broadcast_to(half), ALU.is_equal))
            link(nc.vector.tensor_tensor(past[:, 0:U3, :], oht[:, :, :],
                                         adj[:, :].unsqueeze(1).broadcast_to(half), ALU.mult))
            link(nc.vector.reduce_sum(srow[:, :], past[:, 0:U3, :], AX_X))
            link(nc.vector.tensor_scalar(trow[:, :], tnum[:, 2:], 128.0, float(-DUMMY), ALU.mult, ALU.add))
            link(nc.vector.tensor_tensor(row2[:, :], trow[:, :], valid[:, :], ALU.mult))
            link(nc.vector.tensor_tensor(trow[:, :], row2[:, :], srow[:, :], ALU.add))
            nc.vector.tensor_scalar(tab[:, 0:U3], trow[:, :], float(DUMMY), None, ALU.add).then_inc(t_tab, 1)
            for n in range(1, 4 * EARLY):
                shared_hidden(n, n % 4)
                if n % 4 == 0:
                    take(n // 4 - 1)
            take(EARLY - 1)

            def hidden(n, u):
                tile_done(dve, sg_d, n, u)
                nc.vector.tensor_tensor(h[:, u % 2, :], sg[:, u % 2, :], bank[2 + u % 2][:, H:2 * H],
                                        ALU.mult).then_inc(h_d[u % 4], 1)

            def take_dest(n16, u):
                tile_done(dve, y_sent, n16, u - U3)
                nc.vector.tensor_copy(didx[:, u:u + 1], xin[:, u, D:ROW].bitcast(U32)).then_inc(didx_d[u % 4], 1)

            def result(n, u):
                tile_done(dve, dn_p, n, u)
                nc.vector.tensor_copy(y_sb[:, u % U3, :], bank[6 + u % 2][:, 0:D]).then_inc(y_d[u % 4], 1)

            def body(j, first=False):
                n, n16 = counts(dve, j, U3 // 4), counts(dve, j, dma=True)
                for u in range(U3):
                    hidden(n, u)
                    take_dest(n16, u)
                    if not (first and u < 2):
                        result(n, u - 2)

            body(0, first=True)
            with dve.Fori(1, TG) as j:
                body(j)
            for u in range(2):
                result(counts(dve, TG), u - 2)

            def combine(c, v, k):
                if k == 0:
                    need(dve, yld_in[v], 8 * (c - v) + 16)
                    need(dve, take_d, 4 * c + 4)
                else:
                    need(dve, acc_d, 4 * (TOPK * c + k))
                if k == 1:
                    need(dve, out_sent[v], 8 * (c - v))
                for q in range(4):
                    nc.vector.scalar_tensor_tensor(
                        out=acc[:, v, (k + 1) % 2, q, :], in0=yld[:, v, q, k, :],
                        scalar=gates[:, bass.ds((4 * c + q) * TOPK + k, 1)],
                        in1=acc[:, v, k % 2, q, :] if k else x_all[:, bass.ds((4 * c + q) * D, D)],
                        op0=ALU.mult, op1=ALU.add).then_inc(acc_d, 1)

            def chunk(c, v):
                for u in range(4):
                    shared_hidden(4 * c + u, u)
                    if u == 0:
                        take(c - 1)
                    combine(c - 1, 1 - v, u)

            done = (0, 0, 2, 5, EARLY * TOPK)
            for u in range(4):
                shared_hidden(4 * EARLY + u, u)
                for n in range(done[u], done[u + 1]):
                    combine(n // TOPK, n // TOPK % 2, n % TOPK)
            with dve.Fori(1, CHUNKS // 2 - 1) as j:
                chunk(2 * j + 1, 1)
                chunk(2 * j + 2, 0)
            chunk(CHUNKS - 1, 1)
            take(CHUNKS - 1)
            for k in range(TOPK):
                combine(CHUNKS - 1, 1, k)

        @block.tensor
        def _(pe):
            pe.wait_ge(s_cst, 16)
            pe.wait_ge(s_wkv, 16)
            pe.wait_ge(s_w, 16)
            pe.wait_ge(s_vec, 16)
            pe.wait_ge(s_tri, 2)
            pe.wait_ge(s_zero, 4)

            def step(i, u, has):
                o = 1 - u

                def turn(f):
                    m = i - 1
                    need(pe, exp_d, 3 * m + f + 1)
                    need(pe, pt_d, FILLS * m + f)
                    if f < FILLS - 1:
                        for n in range(4):
                            g, c = divmod(4 * f + n, CH)
                            r = nc.tensor.transpose(ps_p[:, n * T:(n + 1) * T], prob[:, o, g, 128 * c:128 * (c + 1)],
                                                    ident)
                    else:
                        for n in range(NG // 2):
                            two = ptail[:, o, 2 * n:2 * n + 2, :].rearrange("p m k -> p (m k)")
                            r = nc.tensor.transpose(ps_p[:, n * T:(n + 1) * T], two, ident)
                    r.then_inc(pt_p, 1)

                def context(f):
                    m = i - 1
                    need(pe, pt_d, FILLS * m + f + 1)
                    if f == 0:
                        need(pe, vt_d, m + 1)
                        need(pe, on_d, m)
                    if f < FILLS - 1:
                        for n in range(4):
                            g, c = divmod(4 * f + n, CH)
                            near = min(max(g - 1, 0), NG - 3)
                            at = g * GS - (g - near) * GC
                            r = nc.tensor.matmul(ps_o[:, at:at + 3 * GC], pT[:, f, n, :],
                                                 vt[:, o, c, near:near + 3, :].rearrange("p g c -> p (g c)"),
                                                 start=f == 0 and n == 0, stop=False)
                    else:
                        for n in range(NG // 2):
                            r = nc.tensor.matmul(ov[:, 2 * n:2 * n + 2, 0:GC], pT[:, f, n, :], vtail[:, o, n, :, :],
                                                 start=False, stop=n == NG // 2 - 1)
                    r.then_inc(pv_p, 1)

                def keys_values():
                    if has(1):
                        m = i + 1
                        need(pe, ctx_in[o], upto(m, o, 16) + 16)
                        need(pe, vt_d, m)
                        for n in range(2):
                            r = nc.tensor.matmul(ps_f[:, n * NKV:(n + 1) * NKV], wkv_sb[:, n * D:(n + 1) * D], ctx_sb[:, o, :],
                                                 start=True, stop=True)
                        r.then_inc(kv_p, 1)

                if has(0):
                    need(pe, q_d, i + 1)
                    need(pe, kv_d, i + 1)
                    need(pe, diff_d, 2 * i - 1)
                for g in range(NG):
                    if g == 1 and has(-3):
                        need(pe, x2_d, i - 2)
                        need(pe, base_d, i - 3)
                        nc.tensor.transpose(ps_b[:, 0:T], payload[:, o, 0, 0:D], ident).then_inc(x2T_p, 1)
                    if g == 2:
                        keys_values()
                    if g == 2 and has(-1):
                        turn(0)
                    if g == 2 and has(-3):
                        need(pe, x2Ta_d, i - 2)
                        nc.tensor.matmul(ps_b[:, 0:E], x2T[:, :], w[:, W_R:W_R + E], start=True,
                                         stop=True).then_inc(lg_p, 1)
                    if g == 2 and has(0):
                        need(pe, diff_d, 2 * i)
                    if has(0):
                        r = nc.tensor.matmul(bank[g][:, 0:GK], qT[:, u, g, :],
                                             kvbd[:, u, 0, :, :].rearrange("p a k -> p (a k)"), start=True, stop=True)
                        if g % 2:
                            r.then_inc(s_p, 1)
                if has(1):
                    need(pe, kv_d, i + 2)
                    need(pe, xn_d, i + 2)
                    nc.tensor.transpose(ps_f[:, 0:T], xn[:, o, :], ident).then_inc(xnT_p, 1)
                if has(-2):
                    need(pe, on_d, i - 1)
                    need(pe, lg_d, i - 2)
                    nc.tensor.transpose(ps_b[:, 0:T], o_sb[:, :], ident).then_inc(oT_p, 1)

                if has(-1):
                    turn(1)
                if has(1):
                    need(pe, xnT_d, i + 2)
                    nc.tensor.matmul(ps_f[:, 0:T], w[:, W_Q:W_Q + D], xnT[:, o, :], start=True,
                                     stop=True).then_inc(q_p, 1)
                if has(-2):
                    need(pe, oT_d, i - 1)
                    nc.tensor.matmul(ps_b[:, 0:D], oT[:, :], w[:, W_O:W_O + D], start=True, stop=True).then_inc(y_p, 1)
                if has(-1):
                    context(0)
                if has(-1):
                    turn(2)
                if has(-3):
                    m = i - 3
                    need(pe, oh_d, m + 1)
                    need(pe, x1_d, m + 2 if has(-2) else 0)
                    for n, lhs in enumerate((tri, ones)):
                        for k in range(TOPK):
                            r = nc.tensor.matmul(ps_b[:, n * E:(n + 1) * E], lhs[:, :], onehot[:, k, :],
                                                 start=k == 0, stop=k == TOPK - 1)
                    r.then_inc(pre_p, 1)
                if has(1):
                    need(pe, q_d, i + 2)
                    vbd = kvbd[:, o, 1, :, :].rearrange("p a k -> p (a k)")
                    for c in range(CH):
                        nc.tensor.transpose(ps_f[:, c * D:(c + 1) * D], vbd[:, 128 * c:128 * (c + 1)], ident)
                    nc.tensor.transpose(ps_f[0:TAIL, CH * D:(CH + 1) * D], vbd[:, 128 * CH:GK], ident)
                    r = nc.tensor.matmul(ps_f[64:64 + TAIL, CH * D:(CH + 1) * D], vbd[:, 128 * CH:GK], ident,
                                         start=True, stop=True)
                    r.then_inc(vt_p, 1)
                if has(-1):
                    context(1)
                if has(-1):
                    context(2)
            pipeline(pe, step)

            def shared_up(c, n, u):
                need(pe, ssg_d, n - 1)
                need(pe, hs_d, n - 1)
                for which, (at, bk) in enumerate(((W_SG, u % 2), (W_SU, 2 + u % 2))):
                    nc.tensor.matmul(bank[bk][:, :], w[:, at + 128 * u:at + 128 * (u + 1)],
                                     x2T_all[:, bass.ds(c * 512, 512)], start=True, stop=True).then_inc(sg_p, 1)

            def shared_down(n, u):
                need(pe, hs_d, n + 1)
                for q in range(4):
                    if u == 0:
                        need(pe, take_d, n - 4 + q + 1)
                    nc.tensor.matmul(bank[4 + q][:, 0:D], hs[:, u % 2, q * 128:(q + 1) * 128],
                                     w[:, W_SD + 128 * u:W_SD + 128 * (u + 1)], start=u == 0,
                                     stop=u == NS - 1).then_inc(sy_p, 1)

            pe.wait_ge(s_moe, 64)
            pe.wait_ge(base_d, B)
            pe.wait_ge(x2Ta_d, B)
            shared_up(0, 0, 0)
            for n in range(1, 4 * EARLY):
                shared_up(n // 4, n, n % 4)
                shared_down(n - 1, (n - 1) % 4)
            shared_down(4 * EARLY - 1, 3)
            pe.wait_ge(take_d, 4 * EARLY)

            pe.wait_ge(t_load, 16)

            def turn_x(n16, u):
                tile_done(pe, xin_in, n16, u)
                nc.tensor.transpose(bank[u % 2][:, 0:128], xin[:, u % U3, 0:D], ident).then_inc(xT_p[u % 4], 1)

            def gate_up(n, u, e):
                tile_done(pe, xT_d, n, u)
                nc.tensor.matmul(bank[2 + u % 2][:, 0:2 * H], xT[:, u % 2, :], w_gu[:, bass.ds(e * (2 * H), 2 * H)],
                                 start=True, stop=True).then_inc(gu_p[u % 4], 1)

            def turn_h(n, u):
                tile_done(pe, h_d, n, u)
                nc.tensor.transpose(bank[4 + u % 2][:, 0:128], h[:, u % 2, :], ident).then_inc(hT_p[u % 4], 1)

            def down(n, u, e):
                tile_done(pe, hT_d, n, u)
                nc.tensor.matmul(bank[6 + u % 2][:, 0:D], hT[:, u % 2, :], w_dn[:, bass.ds(e * D, D)], start=True,
                                 stop=True).then_inc(dn_p[u % 4], 1)

            def tiles(j, first=False, last=False):
                es = numbers(pe, tab_sb, j * TW + U3, U3 + 2, E - 1)
                n, n16 = counts(pe, j, U3 // 4), counts(pe, j, 2, dma=True)
                for u in range(U3):
                    gate_up(n, u, es[u + 2])
                    if not (first and u == 0):
                        turn_h(n, u - 1)
                    if not (last and u >= U3 - 2):
                        turn_x(n16, u + 2)
                    if not (first and u < 2):
                        down(n, u - 2, es[u])
                return es

            for u in range(2):
                turn_x(counts(pe, 0, 1, dma=True), u)
            tiles(0, first=True)
            with pe.Fori(1, TG - 1) as j:
                tiles(j)
            es = tiles(TG - 1, last=True)
            n = counts(pe, TG - 1, U3 // 4)
            turn_h(n, U3 - 1)
            down(n, U3 - 2, es[U3])
            tile_done(pe, y_d, n, U3 - 3)
            down(n, U3 - 1, es[U3 + 1])

            for u in range(4):
                pe.wait_ge(y_d[u], TILES // 4)
            shared_up(EARLY, 4 * EARLY, 0)
            for u in range(1, 4):
                shared_up(EARLY, 4 * EARLY + u, u)
                shared_down(4 * EARLY + u - 1, u - 1)
            with pe.Fori(EARLY + 1, CHUNKS) as c:
                for u in range(4):
                    shared_up(c, 4 * c + u, u)
                    shared_down(4 * c + u - 1, (u - 1) % 4)
            shared_down(B - 1, 3)


def kernel(**inp):
    import numpy as np
    import concourse.bacc as bacc
    from concourse.bass_utils import run_bass_kernel_spmd as run

    def arr(name):
        return np.asarray(inp[name])

    def rep(v):
        return np.broadcast_to(v, (128, v.size))

    p = np.arange(128)
    f = np.float32
    consts = np.zeros((128, C_END), f)
    consts[:, C_ID:C_ID + 128] = np.eye(128, dtype=f)
    consts[:, C_TRI:C_TRI + 128] = (p[:, None] < p[None, :])
    consts[:, C_ONE:C_ONE + 128] = 1
    consts[:, C_IOTA:C_IOTA + E] = np.arange(E)
    consts[:, C_EOFF:C_EOFF + E] = np.arange(E) * STRIDE
    consts[:, C_T:C_T + U3 + 2] = U3 * p[:, None] + np.arange(-2, U3)
    consts[:, C_DEST:C_DEST + TOPK] = p[:, None] * TOPK + np.arange(TOPK)
    consts[:, C_STEP:C_STEP + TOPK] = T * TOPK
    consts[:, C_PADD] = NOWHERE
    consts[:, C_P] = p
    consts[:, C_MASK:C_MASK + GH] = (p[:, None] // HD % GH == np.arange(GH))
    row = p[:, None] + 128 * np.arange(CH)
    consts[:, C_IND:C_IND + CH * GH] = (row[:, :, None] // NKV == np.arange(GH)).reshape(128, -1)
    for m in range(2):
        head = (128 * CH + np.arange(TAIL)) // NKV
        consts[64 * m:64 * m + TAIL, C_TIND + m * GH:C_TIND + (m + 1) * GH] = head[:, None] == np.arange(GH)
    sd = arr("L0_ffn_sdown_w").T.reshape(NS, 128, D).transpose(1, 0, 2).reshape(128, HS)
    wts = np.concatenate([arr("L0_xattn_Wq"), arr("L0_xattn_Wo"), arr("L0_ffn_router_w").T,
                          arr("L0_ffn_sgate_w").T, arr("L0_ffn_sup_w").T, sd], axis=1)
    vecs = np.concatenate([rep(arr("L0_ffn_router_bias")), rep(arr("L0_xattn_bo")),
                           arr("L0_xattn_bq")[:, None], rep(arr("g_xattn")), rep(arr("g_ffn"))], axis=1)
    ctxT = np.ones((CKV + 1, B * NKV), f)
    ctxT[:CKV] = arr("ctx_768").transpose(2, 0, 1).reshape(CKV, B * NKV)
    wkv = np.concatenate([np.concatenate([arr("L0_xattn_W" + c), arr("L0_xattn_b" + c)[None, :]]) for c in "kv"],
                         axis=1)
    gu = np.concatenate([arr("L0_ffn_gate_w"), arr("L0_ffn_up_w")], axis=1).transpose(2, 0, 1).reshape(D, E * 2 * H)
    dn = arr("L0_ffn_down_w").transpose(2, 0, 1).reshape(H, E * D)
    ins = {
        "x": arr("x"),
        "ctxT": ctxT, "wkv": wkv,
        "wts": wts, "vecs": vecs, "consts": consts, "gu": gu, "dn": dn,
    }
    ins = {k: np.ascontiguousarray(v) for k, v in ins.items()}
    nc = bacc.Bacc("TRN2", target_bir_lowering=False, num_devices=1)
    aps = [nc.dram_tensor(f"in_{k}", v.shape, mybir.dt.from_np(v.dtype), kind="ExternalInput").ap()
           for k, v in ins.items()]
    out = nc.dram_tensor("out", (B, T, D), F32, kind="ExternalOutput").ap()
    build(nc, *aps, out)
    r = run(nc, [{f"in_{k}": v for k, v in ins.items()}], core_ids=[0])
    return r.results[0]["out"]
```
